# Optimizing a Trainium2 kernel written in Bass

```python
import numpy as np
import jax
import jax.numpy as jnp

def _softmax(x, axis=-1):
    return jax.nn.softmax(x, axis=axis)

def _gelu(x):
    return jax.nn.gelu(x, approximate=True)

def _silu(x):
    return jax.nn.silu(x)

def _sigmoid(x):
    return jax.nn.sigmoid(x)

def _layernorm(x, axis=-1, eps=1e-05):
    m = jnp.mean(x, axis=axis, keepdims=True)
    v = jnp.var(x, axis=axis, keepdims=True)
    return (x - m) / jnp.sqrt(v + eps)

def _scatter_add(tgt, idx, src, axis=0):
    return tgt.at[idx].add(src)

def _segment_sum(src, seg, n):
    return jax.ops.segment_sum(src, seg, n)
kernel_name = 'mk_conv_seq_d2_conv_nchw192_r2_9e36c9'

def setup_inputs(seed: int=0):
    np.random.seed(seed)
    _w = jnp.asarray

    def _rec_inputs():
        import jax
        import jax.numpy as jnp
        _gk = jax.random.key(seed)
        x = -0.0002221 + 1 * jax.random.normal(jax.random.fold_in(_gk, 1), (8, 96, 64, 64), jnp.float32)
        return x
    x = _rec_inputs()

    def _L0_conv_setup():
        import jax, jax.numpy as jnp
        import numpy as np
        B, C, H, W = (8, 96, 64, 64)
        K = 17
        PAD = K // 2
        HID = max(C // 4, 32)
        BN_EPS = 1e-05

        def _bn(x, g, b, m, v):
            scale = (g / jnp.sqrt(v + BN_EPS))[None, :, None, None]
            shift = (b - m * g / jnp.sqrt(v + BN_EPS))[None, :, None, None]
            return x * scale + shift
        key = jax.random.key(seed)
        ks = jax.random.split(key, 12)
        x = jax.random.normal(ks[0], (B, C, H, W), dtype=jnp.float32)
        plk_filter = jax.random.normal(ks[1], (C, 1, K, K), dtype=jnp.float32) * 0.05
        bn1_gamma = jnp.ones((C,), jnp.float32)
        bn1_beta = jnp.zeros((C,), jnp.float32)
        bn1_mean = jax.random.normal(ks[2], (C,), dtype=jnp.float32) * 0.1
        bn1_var = jax.random.uniform(ks[3], (C,), jnp.float32, 0.5, 1.5)
        pw_weight = jax.random.normal(ks[4], (C, C), dtype=jnp.float32) * 0.05
        bn2_gamma = jnp.ones((C,), jnp.float32)
        bn2_beta = jnp.zeros((C,), jnp.float32)
        bn2_mean = jax.random.normal(ks[5], (C,), dtype=jnp.float32) * 0.1
        bn2_var = jax.random.uniform(ks[6], (C,), jnp.float32, 0.5, 1.5)
        se_w1 = jax.random.normal(ks[7], (HID, C), dtype=jnp.float32) * 0.05
        se_b1 = jnp.zeros((HID,), jnp.float32)
        se_w2 = jax.random.normal(ks[8], (C, HID), dtype=jnp.float32) * 0.05
        se_b2 = jnp.zeros((C,), jnp.float32)
        gamma = jnp.ones((1,), jnp.float32) * 0.1
        return {'x': x, 'plk_filter': plk_filter, 'bn1_gamma': bn1_gamma, 'bn1_beta': bn1_beta, 'bn1_mean': bn1_mean, 'bn1_var': bn1_var, 'pw_weight': pw_weight, 'bn2_gamma': bn2_gamma, 'bn2_beta': bn2_beta, 'bn2_mean': bn2_mean, 'bn2_var': bn2_var, 'se_w1': se_w1, 'se_b1': se_b1, 'se_w2': se_w2, 'se_b2': se_b2, 'gamma': gamma}
    _L0_conv_all = _L0_conv_setup()
    _L0_conv_in = {k: v for k, v in _L0_conv_all.items() if k in ('plk_filter', 'bn1_gamma', 'bn1_beta', 'bn1_mean', 'bn1_var', 'pw_weight', 'bn2_gamma', 'bn2_beta', 'bn2_mean', 'bn2_var', 'se_w1', 'se_b1', 'se_w2', 'se_b2', 'gamma')}
    del _L0_conv_all

    def _L1_conv_setup():
        import jax, jax.numpy as jnp
        import numpy as np
        DIM = 96
        D_STATE = 16
        D_CONV = 4
        EXPAND = 2
        D_INNER = EXPAND * DIM
        DT_RANK = DIM // 16

        def _silu(x):
            return x * jax.nn.sigmoid(x)

        def _causal_conv(x, w, b):
            L = x.shape[1]
            xp = jnp.pad(x, ((0, 0), (D_CONV - 1, 0), (0, 0)))
            y = sum((xp[:, k:k + L, :] * w[:, k] for k in range(D_CONV)))
            return y + b

        def _selective_scan(x, dt, Bm, Cm, A, D):
            Bsz, L, di = x.shape
            ds = A.shape[1]

            def step(h, inp):
                x_t, dt_t, B_t, C_t = inp
                dA = jnp.exp(dt_t[:, :, None] * A)
                h = dA * h + dt_t[:, :, None] * B_t[:, None, :] * x_t[:, :, None]
                y = jnp.einsum('bds,bs->bd', h, C_t)
                return (h, y)
            h0 = jnp.zeros((Bsz, di, ds), x.dtype)
            xs = (jnp.swapaxes(x, 0, 1), jnp.swapaxes(dt, 0, 1), jnp.swapaxes(Bm, 0, 1), jnp.swapaxes(Cm, 0, 1))
            _, ys = jax.lax.scan(step, h0, xs)
            return jnp.swapaxes(ys, 0, 1) + x * D

        def _mamba(x_seq, W_in, conv_w, conv_b, W_xproj, W_dt, b_dt, A_log, D, W_out):
            xz = x_seq @ W_in
            x, z = (xz[..., :D_INNER], xz[..., D_INNER:])
            x = _silu(_causal_conv(x, conv_w, conv_b))
            proj = x @ W_xproj
            dt = jax.nn.softplus(proj[..., :DT_RANK] @ W_dt + b_dt)
            Bm = proj[..., DT_RANK:DT_RANK + D_STATE]
            Cm = proj[..., DT_RANK + D_STATE:]
            A = -jnp.exp(A_log)
            y = _selective_scan(x, dt, Bm, Cm, A, D)
            return y * _silu(z) @ W_out
        key = jax.random.key(seed)
        ks = jax.random.split(key, 8)
        B, C, H, W = (4, DIM, 32, 32)
        x = jax.random.normal(ks[0], (B, C, H, W), dtype=jnp.float32)
        s_in = 1.0 / np.sqrt(DIM)
        s_xp = 1.0 / np.sqrt(D_INNER)
        s_dt = 1.0 / np.sqrt(DT_RANK)
        params = {'x': x, 'ln_g': jnp.ones((DIM,), jnp.float32), 'ln_b': jnp.zeros((DIM,), jnp.float32), 'W_in': jax.random.normal(ks[1], (DIM, 2 * D_INNER), jnp.float32) * s_in, 'conv_w': jax.random.normal(ks[2], (D_INNER, D_CONV), jnp.float32) * 0.5, 'conv_b': jnp.zeros((D_INNER,), jnp.float32), 'W_xproj': jax.random.normal(ks[3], (D_INNER, DT_RANK + 2 * D_STATE), jnp.float32) * s_xp, 'W_dt': jax.random.normal(ks[4], (DT_RANK, D_INNER), jnp.float32) * s_dt, 'b_dt': jax.random.normal(ks[5], (D_INNER,), jnp.float32) * 0.5 - 4.0, 'A_log': jnp.log(jnp.broadcast_to(jnp.arange(1, D_STATE + 1, dtype=jnp.float32), (D_INNER, D_STATE))) + 0.0, 'D': jnp.ones((D_INNER,), jnp.float32), 'W_out': jax.random.normal(ks[6], (D_INNER, DIM), jnp.float32) * s_xp}
        return params
    _L1_conv_all = _L1_conv_setup()
    _L1_conv_in = {k: v for k, v in _L1_conv_all.items() if k in ('ln_g', 'ln_b', 'W_in', 'conv_w', 'conv_b', 'W_xproj', 'W_dt', 'b_dt', 'A_log', 'D', 'W_out')}
    del _L1_conv_all
    return {'x': x, 'L0_conv_plk_filter': _L0_conv_in['plk_filter'], 'L0_conv_bn1_gamma': _L0_conv_in['bn1_gamma'], 'L0_conv_bn1_beta': _L0_conv_in['bn1_beta'], 'L0_conv_bn1_mean': _L0_conv_in['bn1_mean'], 'L0_conv_bn1_var': _L0_conv_in['bn1_var'], 'L0_conv_pw_weight': _L0_conv_in['pw_weight'], 'L0_conv_bn2_gamma': _L0_conv_in['bn2_gamma'], 'L0_conv_bn2_beta': _L0_conv_in['bn2_beta'], 'L0_conv_bn2_mean': _L0_conv_in['bn2_mean'], 'L0_conv_bn2_var': _L0_conv_in['bn2_var'], 'L0_conv_se_w1': _L0_conv_in['se_w1'], 'L0_conv_se_b1': _L0_conv_in['se_b1'], 'L0_conv_se_w2': _L0_conv_in['se_w2'], 'L0_conv_se_b2': _L0_conv_in['se_b2'], 'L0_conv_gamma': _L0_conv_in['gamma'], 'L1_conv_ln_g': _L1_conv_in['ln_g'], 'L1_conv_ln_b': _L1_conv_in['ln_b'], 'L1_conv_W_in': _L1_conv_in['W_in'], 'L1_conv_conv_w': _L1_conv_in['conv_w'], 'L1_conv_conv_b': _L1_conv_in['conv_b'], 'L1_conv_W_xproj': _L1_conv_in['W_xproj'], 'L1_conv_W_dt': _L1_conv_in['W_dt'], 'L1_conv_b_dt': _L1_conv_in['b_dt'], 'L1_conv_A_log': _L1_conv_in['A_log'], 'L1_conv_D': _L1_conv_in['D'], 'L1_conv_W_out': _L1_conv_in['W_out']}

def reference(x, L0_conv_plk_filter, L0_conv_bn1_gamma, L0_conv_bn1_beta, L0_conv_bn1_mean, L0_conv_bn1_var, L0_conv_pw_weight, L0_conv_bn2_gamma, L0_conv_bn2_beta, L0_conv_bn2_mean, L0_conv_bn2_var, L0_conv_se_w1, L0_conv_se_b1, L0_conv_se_w2, L0_conv_se_b2, L0_conv_gamma, L1_conv_ln_g, L1_conv_ln_b, L1_conv_W_in, L1_conv_conv_w, L1_conv_conv_b, L1_conv_W_xproj, L1_conv_W_dt, L1_conv_b_dt, L1_conv_A_log, L1_conv_D, L1_conv_W_out):
    import jax
    import jax.numpy as jnp

    def _L0_conv_ref(x, plk_filter, bn1_gamma, bn1_beta, bn1_mean, bn1_var, pw_weight, bn2_gamma, bn2_beta, bn2_mean, bn2_var, se_w1, se_b1, se_w2, se_b2, gamma):
        import jax, jax.numpy as jnp
        import numpy as np
        B, C, H, W = (8, 96, 64, 64)
        K = 17
        PAD = K // 2
        HID = max(C // 4, 32)
        BN_EPS = 1e-05

        def _bn(x, g, b, m, v):
            scale = (g / jnp.sqrt(v + BN_EPS))[None, :, None, None]
            shift = (b - m * g / jnp.sqrt(v + BN_EPS))[None, :, None, None]
            return x * scale + shift
        residual = x
        h = _bn(x, bn1_gamma, bn1_beta, bn1_mean, bn1_var)
        h = jax.lax.conv_general_dilated(h, plk_filter, window_strides=(1, 1), padding=[(PAD, PAD), (PAD, PAD)], dimension_numbers=('NCHW', 'OIHW', 'NCHW'), feature_group_count=C)
        h = jnp.einsum('bchw,dc->bdhw', h, pw_weight)
        h = _bn(h, bn2_gamma, bn2_beta, bn2_mean, bn2_var)
        h = jax.nn.gelu(h, approximate=False)
        p = h.mean(axis=(2, 3))
        a = jax.nn.relu(p @ se_w1.T + se_b1)
        a = jax.nn.sigmoid(a @ se_w2.T + se_b2)
        h = h * a[:, :, None, None]
        return residual + gamma * h

    def _L1_conv_ref(x, ln_g, ln_b, W_in, conv_w, conv_b, W_xproj, W_dt, b_dt, A_log, D, W_out):
        import jax, jax.numpy as jnp
        import numpy as np
        DIM = 96
        D_STATE = 16
        D_CONV = 4
        EXPAND = 2
        D_INNER = EXPAND * DIM
        DT_RANK = DIM // 16

        def _silu(x):
            return x * jax.nn.sigmoid(x)

        def _causal_conv(x, w, b):
            L = x.shape[1]
            xp = jnp.pad(x, ((0, 0), (D_CONV - 1, 0), (0, 0)))
            y = sum((xp[:, k:k + L, :] * w[:, k] for k in range(D_CONV)))
            return y + b

        def _selective_scan(x, dt, Bm, Cm, A, D):
            Bsz, L, di = x.shape
            ds = A.shape[1]

            def step(h, inp):
                x_t, dt_t, B_t, C_t = inp
                dA = jnp.exp(dt_t[:, :, None] * A)
                h = dA * h + dt_t[:, :, None] * B_t[:, None, :] * x_t[:, :, None]
                y = jnp.einsum('bds,bs->bd', h, C_t)
                return (h, y)
            h0 = jnp.zeros((Bsz, di, ds), x.dtype)
            xs = (jnp.swapaxes(x, 0, 1), jnp.swapaxes(dt, 0, 1), jnp.swapaxes(Bm, 0, 1), jnp.swapaxes(Cm, 0, 1))
            _, ys = jax.lax.scan(step, h0, xs)
            return jnp.swapaxes(ys, 0, 1) + x * D

        def _mamba(x_seq, W_in, conv_w, conv_b, W_xproj, W_dt, b_dt, A_log, D, W_out):
            xz = x_seq @ W_in
            x, z = (xz[..., :D_INNER], xz[..., D_INNER:])
            x = _silu(_causal_conv(x, conv_w, conv_b))
            proj = x @ W_xproj
            dt = jax.nn.softplus(proj[..., :DT_RANK] @ W_dt + b_dt)
            Bm = proj[..., DT_RANK:DT_RANK + D_STATE]
            Cm = proj[..., DT_RANK + D_STATE:]
            A = -jnp.exp(A_log)
            y = _selective_scan(x, dt, Bm, Cm, A, D)
            return y * _silu(z) @ W_out
        B, C, H, W = x.shape
        xh = jnp.transpose(x, (0, 2, 3, 1))
        mu = xh.mean(-1, keepdims=True)
        var = xh.var(-1, keepdims=True)
        xn = (xh - mu) * jax.lax.rsqrt(var + 1e-05) * ln_g + ln_b
        x_seq = xn.reshape(B, H * W, C)
        mparams = (W_in, conv_w, conv_b, W_xproj, W_dt, b_dt, A_log, D, W_out)
        out_fwd = _mamba(x_seq, *mparams)
        out_bwd = jnp.flip(_mamba(jnp.flip(x_seq, 1), *mparams), 1)
        out = out_fwd + out_bwd
        return jnp.transpose(out, (0, 2, 1)).reshape(B, C, H, W)

    def _gn(v, G=32, eps=1e-05):
        B_, C_, H_, W_ = v.shape
        g = v.reshape(B_, G, C_ // G, H_, W_)
        m = jnp.mean(g, axis=(2, 3, 4), keepdims=True)
        s = jnp.var(g, axis=(2, 3, 4), keepdims=True)
        return ((g - m) / jnp.sqrt(s + eps)).reshape(v.shape)

    def _ln_c(v, eps=1e-06):
        m = jnp.mean(v, axis=1, keepdims=True)
        s = jnp.var(v, axis=1, keepdims=True)
        return (v - m) / jnp.sqrt(s + eps)

    def _ln_t(v, eps=1e-05):
        m = jnp.mean(v, axis=-1, keepdims=True)
        s = jnp.var(v, axis=-1, keepdims=True)
        return (v - m) / jnp.sqrt(s + eps)

    def _to_tokens(v):
        B_, C_, H_, W_ = v.shape
        return v.reshape(B_, C_, H_ * W_).transpose(0, 2, 1)

    def _from_tokens(t, like):
        B_, C_, H_, W_ = like.shape
        return t.transpose(0, 2, 1).reshape(B_, C_, H_, W_)
    x = _L0_conv_ref(x, L0_conv_plk_filter, L0_conv_bn1_gamma, L0_conv_bn1_beta, L0_conv_bn1_mean, L0_conv_bn1_var, L0_conv_pw_weight, L0_conv_bn2_gamma, L0_conv_bn2_beta, L0_conv_bn2_mean, L0_conv_bn2_var, L0_conv_se_w1, L0_conv_se_b1, L0_conv_se_w2, L0_conv_se_b2, L0_conv_gamma)
    x = _L1_conv_ref(x, L1_conv_ln_g, L1_conv_ln_b, L1_conv_W_in, L1_conv_conv_w, L1_conv_conv_b, L1_conv_W_xproj, L1_conv_W_dt, L1_conv_b_dt, L1_conv_A_log, L1_conv_D, L1_conv_W_out)
    return x

_drawn_inputs = setup_inputs


def setup_inputs(seed=0):
    import zlib

    import numpy as np

    out = dict(_drawn_inputs(seed))
    spreads = {'L0_conv_bn1_gamma': (1.0, 0.6),
     'L0_conv_bn1_beta': (0.0, 0.8),
     'L0_conv_bn2_gamma': (1.0, 0.6),
     'L0_conv_bn2_beta': (0.0, 0.8),
     'L0_conv_se_b1': (0.0, 0.8),
     'L0_conv_se_b2': (0.0, 0.8),
     'L1_conv_ln_g': (1.0, 0.2),
     'L1_conv_ln_b': (0.0, 0.1),
     'L1_conv_conv_b': (0.0, 0.1),
     'L1_conv_D': (1.0, 0.2)}
    factors = {'L0_conv_plk_filter': 3.145,
     'L0_conv_bn1_mean': 8.0,
     'L0_conv_bn1_var': 8.0,
     'L0_conv_pw_weight': 3.112,
     'L0_conv_bn2_mean': 8.0,
     'L0_conv_bn2_var': 8.0,
     'L0_conv_se_w1': 8.0,
     'L0_conv_se_w2': 8.0}
    for name, (base, spread) in spreads.items():
        noise = np.random.default_rng([zlib.crc32(name.encode()), seed]).standard_normal(out[name].shape)
        drawn = base * np.exp(spread * noise) if base else spread * noise
        out[name] = jnp.asarray(drawn.astype(out[name].dtype))
    for name, factor in factors.items():
        out[name] = (out[name] * factor).astype(out[name].dtype)
    return out
```

```python
from contextlib import ExitStack

import concourse.bass as bass
from concourse import mybir

F32 = mybir.dt.float32
BF16 = mybir.dt.bfloat16
ALU = mybir.AluOpType
ACT = mybir.ActivationFunctionType
AX_X = mybir.AxisListType.X

P = 128
B, C, H, W = 8, 96, 64, 64
L = H * W
BN_EPS = 1e-5
LN_EPS = 1e-5

K = 17
PAD = K // 2
XH = W // 2
SHIFTS = PAD + 1
NEAR = PAD // 2
XP = XH + 2 * NEAR
CB = 4
BATCHES = C // CB
FCOLS = SHIFTS * 2
FROWS = 2 * K
YG = 4
NYG = H // YG

DI = 192
HALF = DI // 2
DS = 16
DR = 6
DCONV = 4
T = 1024
SL = 512
CHUNKS = L // T
HALO = DCONV - 1
XN = T + 2 * HALO
GC = P // DS
UNITS = DI // GC
HU = UNITS // 2
QN = 32 // GC
ITERS = B * CHUNKS
LEAD = 4


def upper(ap):
    return ap.bitcast(BF16)[:, 1::2]



def wait(eng, sem, count, when=True):
    if when is True or not isinstance(when, (bool, int)) or when:
        eng.wait_ge(sem, count)


def convolution(nc, d, hs):
    with ExitStack() as ctx:
        def sb(name, shape, dt=F32):
            return ctx.enter_context(nc.sbuf_tensor(name, shape, dt))

        def sem(name):
            return ctx.enter_context(nc.semaphore(name))

        filt = sb("filt", [3 * FROWS, (C + CB) * FCOLS])
        filt_tmp = hs[0:3 * FROWS, 0:C * FCOLS]
        masks = sb("masks", [3 * FROWS, 2])
        band_f = sb("band_f", [3 * FROWS, 2 * (2 * H - 1)])
        band = sb("band", [3 * FROWS, 2, 2 * H - 1], BF16)
        bands = sb("bands", [3 * FROWS, H, P], BF16)
        toep = [sb(f"toep{i}", [P, CB * FCOLS, H]) for i in range(2)]
        xraw = [sb(f"xraw{i}", [P, CB, B, XH]) for i in range(2)]
        xpad = [sb(f"xpad{i}", [P, CB, B, XP]) for i in range(2)]
        bnp = sb("bnp", [P, 4, C])
        bnt = sb("bnt", [P, 3, C])
        scale = sb("scale", [P, C])
        shift = sb("shift", [P, C])
        eps = sb("eps", [P, 1])
        pw = [ctx.enter_context(nc.psum_tensor(f"pw{i}", [P, SL], F32)) for i in range(2)]
        pc = [ctx.enter_context(nc.psum_tensor(f"pc{i}", [P, SL], F32)) for i in range(CB)]

        const_in = sem("const_in")
        x_in = [sem(f"x_in{i}") for i in range(2)]
        eps_set = sem("eps_set")
        bn_sqrt = sem("bn_sqrt")
        bn_dve = sem("bn_dve")
        filt_step = sem("filt_step")
        band_ready = sem("band_ready")
        pads_zero = sem("pads_zero")
        x_ready = sem("x_ready")
        w_ready = sem("w_ready")
        w_evac = [sem(f"w_evac{i}") for i in range(2)]
        conv_done = [sem(f"conv_done{i}") for i in range(2)]
        h_evac = [sem(f"h_evac{i}") for i in range(CB)]

        xk = d["x_cols"]
        NCONST = 3 + 3 + 4
        after = [range(NYG // CB * i, NYG // CB * (i + 1)) for i in range(CB)]

        with nc.Block() as block:
            @block.sync
            def _(sp):
                for i in range(2):
                    sp.dma_start(xraw[i][:, :, :, :], xk[:, i * CB:(i + 1) * CB, :, :]).then_inc(x_in[i], 16)
                for i in range(3):
                    sp.dma_start(filt[i * FROWS:(i + 1) * FROWS, 0:C * FCOLS], d["filter_cols"]).then_inc(const_in, 16)
                sp.dma_start(band_f[:, :], d["band"]).then_inc(const_in, 16)
                sp.dma_start(masks[:, :], d["split_masks"]).then_inc(const_in, 16)
                for i, name in enumerate(("gamma", "beta", "mean", "var")):
                    sp.dma_start(bnp[:, i, :], d["bn1_" + name].partition_broadcast(P)).then_inc(const_in, 16)
                with sp.Fori(0, BATCHES // 2) as i:
                    for par in range(2):
                        ch = (2 * i + par + 2) % BATCHES * CB
                        sp.wait_ge(x_ready, 2 * i + par + 1)
                        sp.dma_start(xraw[par][:, :, :, :], xk[:, bass.ds(ch, CB), :, :]).then_inc(x_in[par], 16)
                for i in range(2):
                    sp.wait_ge(x_in[i], 16 * (BATCHES // 2 + 1))

            @block.gpsimd
            def _(pool):
                for i in range(2):
                    nc.gpsimd.memset(xpad[i][:, :, :, 0:NEAR], 0.0)
                    last = nc.gpsimd.memset(xpad[i][:, :, :, NEAR + XH:XP], 0.0)
                last.then_inc(pads_zero, 1)

            def evacuate_weights(eng, copy, s, buf, bank, yg, batches_before):
                if batches_before is not None:
                    eng.wait_ge(conv_done[buf], CB * batches_before)
                eng.wait_ge(w_ready, NYG * s + yg + 1)
                src = pw[bank][:, 0:YG * CB * FCOLS].rearrange("p (y n) -> p n y", y=YG)
                copy(toep[buf][:, :, yg * YG:(yg + 1) * YG], src).then_inc(w_evac[bank], 1)

            def evacuate_conv(eng, copy, i, par, c):
                s = 2 * i + par
                eng.wait_ge(conv_done[par], CB * i + c + 1)
                copy(hs[:, bass.ds((CB * s + c) * B * XH, B * XH)], pc[c][:, 0:B * XH]).then_inc(h_evac[c], 1)

            def evacuations(eng, copy, mine, norm=None):
                for yg in range(mine, NYG, 2):
                    evacuate_weights(eng, copy, 0, 0, mine, yg, None)
                with eng.Fori(0, BATCHES // 2) as i:
                    for par in range(2):
                        s = 2 * i + par
                        for c in range(CB):
                            if c % 2 == mine:
                                evacuate_conv(eng, copy, i, par, c)
                            for yg in after[c]:
                                if yg % 2 == mine:
                                    evacuate_weights(eng, copy, s + 1, 1 - par, mine, yg, i + par)
                            if norm and c == 1:
                                norm(i, par)

            @block.scalar
            def _(act):
                act.wait_ge(const_in, 16 * (NCONST - 1))
                act.wait_ge(eps_set, 1)
                nc.scalar.activation(bnt[:, 0, :], bnp[:, 3, :], ACT.Sqrt, bias=eps[:, 0:1]).then_inc(bn_sqrt, 1)
                evacuations(act, nc.scalar.copy, 0)

            @block.vector
            def _(dve):
                nc.vector.memset(filt[:, C * FCOLS:], 0.0)
                nc.vector.memset(eps[:, :], BN_EPS).then_inc(eps_set, 1)
                dve.wait_ge(const_in, 16 * (NCONST - 1))
                nc.vector.tensor_copy(band[:, :, :].rearrange("p a b -> p (a b)"), band_f[:, :]).then_inc(band_ready, 1)
                dve.wait_ge(band_ready, 1)
                for y in range(H):
                    last = nc.vector.tensor_copy(bands[:, y, :].rearrange("p (a b) -> p a b", a=2), band[:, :, H - 1 - y:2 * H - 1 - y])
                last.then_inc(band_ready, 1)
                f = filt[:, 0:C * FCOLS]
                nc.vector.scalar_tensor_tensor(filt_tmp, upper(f), masks[:, 0:1], f, ALU.mult, ALU.add).then_inc(filt_step, 1)
                dve.wait_ge(filt_step, 1)
                nc.vector.scalar_tensor_tensor(f, upper(filt_tmp), masks[:, 1:2], filt_tmp, ALU.mult, ALU.add).then_inc(filt_step, 1)
                dve.wait_ge(bn_sqrt, 1)
                nc.vector.reciprocal(bnt[:, 1, :], bnt[:, 0, :]).then_inc(bn_dve, 1)
                dve.wait_ge(bn_dve, 1)
                nc.vector.tensor_tensor(scale[:, :], bnt[:, 1, :], bnp[:, 0, :], ALU.mult).then_inc(bn_dve, 1)
                dve.wait_ge(bn_dve, 2)
                nc.vector.tensor_tensor(bnt[:, 2, :], scale[:, :], bnp[:, 2, :], ALU.mult).then_inc(bn_dve, 1)
                dve.wait_ge(bn_dve, 3)
                nc.vector.tensor_tensor(shift[:, :], bnp[:, 1, :], bnt[:, 2, :], ALU.subtract).then_inc(bn_dve, 2)
                dve.wait_ge(filt_step, 2)
                dve.wait_ge(bn_dve, 5)
                dve.wait_ge(pads_zero, 1)

                def batch_norm(s, buf, loads):
                    dve.wait_ge(x_in[buf], 16 * loads)
                    for c in range(CB):
                        at = s * CB + c
                        last = nc.vector.tensor_scalar(xpad[buf][:, c, :, NEAR:NEAR + XH], xraw[buf][:, c, :, :],
                                                       scale[:, bass.ds(at, 1)], shift[:, bass.ds(at, 1)], ALU.mult, ALU.add)
                    last.then_inc(x_ready, 1)

                def next_norm(i, par):
                    wait(dve, conv_done[1 - par], CB * (i + par), True)
                    batch_norm((2 * i + par + 1) % BATCHES, 1 - par, i + par + 1)

                batch_norm(0, 0, 1)
                evacuations(dve, nc.vector.tensor_copy, 1, next_norm)

            @block.tensor
            def _(pe):
                pe.wait_ge(filt_step, 2)
                pe.wait_ge(band_ready, 2)

                def weights(s, yg):
                    bank = yg % 2
                    pe.wait_ge(w_evac[bank], (NYG // 2) * s + yg // 2)
                    for r in range(YG):
                        y = yg * YG + r
                        last = nc.tensor.matmul(pw[bank][:, r * CB * FCOLS:(r + 1) * CB * FCOLS],
                                                bands[:, y, :],
                                                filt[:, bass.ds(s * (CB * FCOLS), CB * FCOLS)].bitcast(BF16)[:, 1::2],
                                                start=True, stop=True, skip_group_check=True)
                    last.then_inc(w_ready, 1)

                for yg in range(NYG):
                    weights(0, yg)
                pe.wait_ge(pads_zero, 1)
                with pe.Fori(0, BATCHES // 2) as i:
                    for par in range(2):
                        s = 2 * i + par
                        pe.wait_ge(x_ready, s + 1)
                        for bank in range(2):
                            pe.wait_ge(w_evac[bank], (NYG // 2) * (s + 1))
                        for c in range(CB):
                            pe.wait_ge(h_evac[c], s)
                            for k in range(SHIFTS):
                                n0 = (c * SHIFTS + k) * 2
                                last = nc.tensor.matmul(pc[c][:, 0:B * XH].rearrange("p (b x) -> p b x", b=B),
                                                        toep[par][:, n0:n0 + 2, :].rearrange("p a y -> p (a y)"),
                                                        xpad[par][:, c, :, k:k + XH],
                                                        start=(k == 0), stop=(k == SHIFTS - 1))
                            last.then_inc(conv_done[par], 1)
                            for yg in after[c]:
                                weights(s + 1, yg)


def pointwise(nc, d, hs, gate):
    with ExitStack() as ctx:
        def sb(name, shape, dt=F32):
            return ctx.enter_context(nc.sbuf_tensor(name, shape, dt))

        def sem(name):
            return ctx.enter_context(nc.semaphore(name))

        HID = 32
        GROUPS = B * XH // 4
        GPB = GROUPS // B
        ident = sb("ident", [P, P])
        wpw = sb("wpw", [C, C])
        se1 = sb("se1", [C, HID])
        se2 = sb("se2", [HID, C])
        b1 = sb("b1", [HID, 1])
        b2 = sb("b2", [C, 1])
        gam = sb("gam", [C, 1])
        bn = sb("bn", [C, 4])
        bt = sb("bt", [C, 5])
        ht = [sb(f"ht{i}", [C, SL]) for i in range(2)]
        act_out = [sb(f"act_out{i}", [C, H, W]) for i in range(2)]
        sums = sb("sums", [C, GROUPS])
        mean = sb("mean", [C, B])
        hid = sb("hid", [HID, B])
        sig = sb("sig", [C, B])
        pt = [ctx.enter_context(nc.psum_tensor(f"pt{i}", [P, SL], F32)) for i in range(2)]
        pp = [ctx.enter_context(nc.psum_tensor(f"pp{i}", [P, SL], F32)) for i in range(2)]
        ps = [ctx.enter_context(nc.psum_tensor(f"ps{i}", [P, SL], F32)) for i in range(2)]

        p_in = sem("p_in")
        bn_s = sem("bn_s")
        bn_v = sem("bn_v")
        turned = sem("turned")
        t_evac = sem("t_evac")
        mixed = sem("mixed")
        gelu_done = sem("gelu_done")
        g_out = [sem(f"g_out{i}") for i in range(2)]
        se_mean = sem("se_mean")
        se_hid = sem("se_hid")
        se_relu = sem("se_relu")
        se_out = sem("se_out")
        se_sig = sem("se_sig")
        loads = [(ident[:, :], d["ident"]), (wpw[:, :], d["pw_t"]), (se1[:, :], d["se_w1_t"]), (se2[:, :], d["se_w2_t"]),
                 (b1[:, :], d["se_b1"].unsqueeze(1)), (b2[:, :], d["se_b2"].unsqueeze(1)),
                 (gam[:, :], d["gamma"].partition_broadcast(C))]
        loads += [(bn[:, i:i + 1], d["bn2_" + n].unsqueeze(1)) for i, n in enumerate(("gamma", "beta", "mean", "var"))]

        with nc.Block() as block:
            @block.sync
            def _(sp):
                for dst, src in loads:
                    sp.dma_start(dst, src).then_inc(p_in, 16)
                for b in range(B):
                    sp.wait_ge(gelu_done, GPB * (b + 1))
                    sp.dma_start(d["act_scr"][b], act_out[b % 2][:, :, :].rearrange("c y x -> c (y x)")).then_inc(g_out[b % 2], 16)
                for i in range(2):
                    sp.wait_ge(g_out[i], 16 * (B // 2))

            @block.tensor
            def _(pe):
                pe.wait_ge(p_in, 16 * len(loads))

                def mix(g):
                    pe.wait_ge(t_evac, g + 1)
                    if g >= 2:
                        pe.wait_ge(gelu_done, g - 1)
                    nc.tensor.matmul(pp[g % 2][0:C, :], wpw[:, :], ht[g % 2][:, :], start=True, stop=True).then_inc(mixed, 1)

                for g in range(GROUPS):
                    if g >= 2:
                        pe.wait_ge(t_evac, g - 1)
                    for r in range(4):
                        last = nc.tensor.transpose(pt[g % 2][0:C, r * P:(r + 1) * P],
                                                   hs[:, :].rearrange("p (c n) -> p c n", c=C)[:, :, 4 * g + r], ident[:, :])
                    last.then_inc(turned, 1)
                    if g >= 1:
                        mix(g - 1)
                mix(GROUPS - 1)
                pe.wait_ge(se_mean, 2)
                nc.tensor.matmul(ps[0][0:HID, 0:B], se1[:, :], mean[:, :], start=True, stop=True).then_inc(se_hid, 1)
                pe.wait_ge(se_relu, 1)
                nc.tensor.matmul(ps[1][0:C, 0:B], se2[:, :], hid[:, :], start=True, stop=True).then_inc(se_out, 1)

            @block.vector
            def _(dve):
                nc.vector.memset(bt[:, 4:5], BN_EPS).then_inc(bn_s, 1)
                dve.wait_ge(bn_s, 2)
                nc.vector.reciprocal(bt[:, 1:2], bt[:, 0:1]).then_inc(bn_v, 1)
                dve.wait_ge(bn_v, 1)
                nc.vector.tensor_tensor(bt[:, 2:3], bt[:, 1:2], bn[:, 0:1], ALU.mult).then_inc(bn_v, 1)
                dve.wait_ge(bn_v, 2)
                nc.vector.tensor_tensor(bt[:, 1:2], bt[:, 2:3], bn[:, 2:3], ALU.mult).then_inc(bn_v, 1)
                dve.wait_ge(bn_v, 3)
                nc.vector.tensor_tensor(bt[:, 3:4], bn[:, 1:2], bt[:, 1:2], ALU.subtract).then_inc(bn_v, 1)
                for g in range(GROUPS):
                    dve.wait_ge(turned, g + 1)
                    if g >= 2:
                        dve.wait_ge(mixed, g - 1)
                    nc.vector.tensor_copy(ht[g % 2][:, :], pt[g % 2][0:C, :]).then_inc(t_evac, 1)
                dve.wait_ge(gelu_done, GROUPS)
                nc.vector.tensor_reduce(mean[:, :], sums[:, :].rearrange("c (b g) -> c b g", b=B), AX_X, ALU.add).then_inc(se_mean, 1)
                dve.wait_ge(se_mean, 1)
                nc.vector.tensor_scalar(mean[:, :], mean[:, :], 1.0 / L, None, ALU.mult).then_inc(se_mean, 1)
                dve.wait_ge(se_sig, 1)
                nc.vector.tensor_scalar(gate[:, :], sig[:, :], gam[:, 0:1], None, ALU.mult)

            @block.scalar
            def _(act):
                act.wait_ge(p_in, 16 * len(loads))
                act.wait_ge(bn_s, 1)
                nc.scalar.activation(bt[:, 0:1], bn[:, 3:4], ACT.Sqrt, bias=bt[:, 4:5]).then_inc(bn_s, 1)
                act.wait_ge(bn_v, 4)
                for g in range(GROUPS):
                    b, col = g // GPB, g % GPB
                    if b >= 2 and col == 0:
                        act.wait_ge(g_out[b % 2], 16 * (b // 2))
                    act.wait_ge(mixed, g + 1)
                    nc.scalar.activation(act_out[b % 2][:, :, 8 * col:8 * col + 8].rearrange("c y x -> c x y"),
                                         pp[g % 2][0:C, :].rearrange("c (x y) -> c x y", y=H), ACT.Gelu,
                                         bias=bt[:, 3:4], scale=bt[:, 2:3], accum_out=sums[:, g:g + 1]).then_inc(gelu_done, 1)
                act.wait_ge(se_hid, 1)
                nc.scalar.activation(hid[:, :], ps[0][0:HID, 0:B], ACT.Relu, bias=b1[:, 0:1]).then_inc(se_relu, 1)
                act.wait_ge(se_out, 1)
                nc.scalar.activation(sig[:, :], ps[1][0:C, 0:B], ACT.Sigmoid, bias=b2[:, 0:1]).then_inc(se_sig, 1)


def normalise(nc, d, gate):
    NS = L // SL
    RING = 4
    with ExitStack() as ctx:
        def sb(name, shape, dt=F32):
            return ctx.enter_context(nc.sbuf_tensor(name, shape, dt))

        def sem(name):
            return ctx.enter_context(nc.semaphore(name))

        averager = sb("averager", [C, C])
        lng = sb("lng", [C, 2])
        eps = sb("ln_eps", [C, 1])
        zero = sb("zero", [C, B, HALO])
        h_in = sb("h_in", [C, RING, SL])
        x_in = sb("x_in_ln", [C, RING, SL])
        x1 = sb("x1", [C, RING, SL])
        xc = sb("xc_ln", [C, RING, SL])
        sq = sb("sq", [C, RING, SL])
        sd = sb("sd", [C, RING, SL])
        rs = sb("rs", [C, RING, SL])
        xs = sb("xs", [C, RING, SL])
        xo = sb("xo", [C, RING, SL])
        pm = [ctx.enter_context(nc.psum_tensor(f"pm{i}", [P, SL], F32)) for i in range(2)]
        pv = [ctx.enter_context(nc.psum_tensor(f"pv{i}", [P, SL], F32)) for i in range(2)]
        ln_const = sem("ln_const")
        ln_set = sem("ln_set")
        loaded = [sem(f"ln_loaded{i}") for i in range(RING)]
        stored = [sem(f"ln_stored{i}") for i in range(RING)]
        halo = sem("halo")
        added = sem("added")
        mean_ready = sem("mean_ready")
        centred = sem("centred")
        squared = sem("squared")
        var_ready = sem("var_ready")
        sd_ready = sem("sd_ready")
        rs_ready = sem("rs_ready")
        scaled = sem("scaled")
        affine = sem("affine")
        xn = d["xn_scr"]

        with nc.Block() as block:
            @block.sync
            def _(sp):
                sp.dma_start(averager[:, :], d["averager"]).then_inc(ln_const, 16)
                sp.dma_start(lng[:, 0:1], d["ln_g"].unsqueeze(1)).then_inc(ln_const, 16)
                sp.dma_start(lng[:, 1:2], d["ln_b"].unsqueeze(1)).then_inc(ln_const, 16)
                sp.wait_ge(ln_set, 1)
                sp.dma_start(xn[:, :, 0:HALO].rearrange("b c t -> c b t"), zero[:, :, :]).then_inc(halo, 16)
                sp.dma_start(xn[:, :, HALO + L:].rearrange("b c t -> c b t"), zero[:, :, :]).then_inc(halo, 16)
                with sp.Fori(0, B) as b:
                    for s in range(NS):
                        r = s % RING
                        wait(sp, added, NS * b + s - RING + 1, s >= RING - 1)
                        if s < RING - 1:
                            sp.wait_ge(added, NS * b)
                        sp.dma_start(h_in[:, r, :], d["act_scr"][b, :, s * SL:(s + 1) * SL]).then_inc(loaded[r], 16)
                        sp.dma_start(x_in[:, r, :], d["x_tok"][b, :, s * SL:(s + 1) * SL]).then_inc(loaded[r], 16)
                sp.wait_ge(halo, 32)
                for r in range(RING):
                    sp.wait_ge(stored[r], 16 * (B * NS // RING))

            @block.vector
            def _(dve):
                nc.vector.memset(eps[:, :], LN_EPS)
                nc.vector.memset(zero[:, :, :], 0.0).then_inc(ln_set, 1)

                def add(b, s):
                    r = s % RING
                    dve.wait_ge(loaded[r], 32 * (NS // RING * b + s // RING + 1))
                    wait(dve, mean_ready, NS * b + s - RING + 1, s >= RING)
                    nc.vector.scalar_tensor_tensor(x1[:, r, :], h_in[:, r, :], gate[:, bass.ds(b, 1)], x_in[:, r, :],
                                                   ALU.mult, ALU.add).then_inc(added, 1)

                def centre(b, s):
                    r = s % RING
                    dve.wait_ge(mean_ready, NS * b + s + 1)
                    dve.wait_ge(added, NS * b + s + 1)
                    wait(dve, scaled, NS * b + s - RING + 1, s >= RING)
                    nc.vector.tensor_tensor(xc[:, r, :], x1[:, r, :], pm[s % 2][0:C, :], ALU.subtract).then_inc(centred, 1)

                def invert(b, s):
                    r = s % RING
                    dve.wait_ge(sd_ready, NS * b + s + 1)
                    nc.vector.reciprocal(rs[:, r, :], sd[:, r, :]).then_inc(rs_ready, 1)

                with dve.Fori(0, B) as b:
                    dve.wait_ge(scaled, NS * b)
                    for s in range(NS + 3):
                        if s < NS:
                            add(b, s)
                        if 1 <= s <= NS:
                            centre(b, s - 1)
                        if s >= 3:
                            invert(b, s - 3)

            @block.tensor
            def _(pe):
                pe.wait_ge(ln_const, 48)
                with pe.Fori(0, B) as b:
                    pe.wait_ge(sd_ready, NS * b)
                    for s in range(NS + 2):
                        if s < NS:
                            pe.wait_ge(added, NS * b + s + 1)
                            wait(pe, centred, NS * b + s - 1, s >= 2)
                            nc.tensor.matmul(pm[s % 2][0:C, :], averager[:, :], x1[:, s % RING, :], start=True, stop=True).then_inc(mean_ready, 1)
                        if s >= 2:
                            v = s - 2
                            pe.wait_ge(squared, NS * b + v + 1)
                            wait(pe, sd_ready, NS * b + v - 1, v >= 2)
                            nc.tensor.matmul(pv[v % 2][0:C, :], averager[:, :], sq[:, v % RING, :], start=True, stop=True).then_inc(var_ready, 1)

            @block.scalar
            def _(act):
                act.wait_ge(ln_set, 1)
                act.wait_ge(ln_const, 48)
                with act.Fori(0, B) as b:
                    for s in range(NS + 4):
                        if 1 <= s <= NS:
                            v = s - 1
                            act.wait_ge(centred, NS * b + v + 1)
                            wait(act, var_ready, NS * b + v - RING + 1, v >= RING)
                            nc.scalar.activation(sq[:, v % RING, :], xc[:, v % RING, :], ACT.Square).then_inc(squared, 1)
                        if 2 <= s <= NS + 1:
                            v = s - 2
                            act.wait_ge(var_ready, NS * b + v + 1)
                            wait(act, rs_ready, NS * b + v - RING + 1, v >= RING)
                            nc.scalar.activation(sd[:, v % RING, :], pv[v % 2][0:C, :], ACT.Sqrt, bias=eps[:, 0:1]).then_inc(sd_ready, 1)
                        if s >= 4:
                            v = s - 4
                            r = v % RING
                            act.wait_ge(scaled, NS * b + v + 1)
                            act.wait_ge(stored[r], 16 * (NS // RING * b + v // RING))
                            nc.scalar.activation(xo[:, r, :], xs[:, r, :], ACT.Identity, bias=lng[:, 1:2], scale=lng[:, 0:1]).then_inc(affine, 1)
                            act.wait_ge(affine, NS * b + v + 1)
                            act.dma_start(xn[b, :, HALO + v * SL:HALO + (v + 1) * SL], xo[:, r, :]).then_inc(stored[r], 16)

            @block.gpsimd
            def _(pool):
                with pool.Fori(0, B) as b:
                    for s in range(NS):
                        r = s % RING
                        pool.wait_ge(rs_ready, NS * b + s + 1)
                        pool.wait_ge(centred, NS * b + s + 1)
                        wait(pool, affine, NS * b + s - RING + 1, s >= RING)
                        if s == 0:
                            pool.wait_ge(affine, NS * b)
                        nc.gpsimd.tensor_tensor(xs[:, r, :], xc[:, r, :], rs[:, r, :], ALU.mult).then_inc(scaled, 1)


def weights(nc, d, w):
    with ExitStack() as ctx:
        def sb(name, shape, dt=F32):
            return ctx.enter_context(nc.sbuf_tensor(name, shape, dt))

        def sem(name):
            return ctx.enter_context(nc.semaphore(name))

        w_in = sb("w_in", [HALF, DI])
        taps = sb("taps", [HALF, DCONV, DI])
        wx = sb("wx", [HALF, 2, DR + 2 * DS])
        wx_t = sb("wx_t", [DR, DI])
        wdt = sb("wdt", [DR, DI])
        spread_f = sb("spread_f", [HALF, QN * P])
        pd = [ctx.enter_context(nc.psum_tensor(f"pd{i}", [P, SL], F32)) for i in range(2)]
        w_loaded = sem("w_loaded")
        w_prod = sem("w_prod")
        a_exp = sem("a_exp")
        loads = [(w_in[:, :], d["w_in"][:, 0:DI]), (w["z"][:, :], d["w_in"][:, DI:2 * DI]),
                 (taps[:, :, :].rearrange("c k n -> c (k n)"), d["conv_taps"].partition_broadcast(HALF)),
                 (wx[:, :, :], d["w_x"]), (wx_t[:, :], d["w_x_t"]), (wdt[:, :], d["w_dt"]),
                 (spread_f[:, :], d["spread"]), (w["gather"][:, :, :].rearrange("p q n -> p (q n)"), d["gather"]),
                 (w["a"][:, :], d["a_log"]), (w["out"][:, :, :], d["w_out"]),
                 (w["conv_b"][:, :], d["conv_b"]), (w["dt_b"][:, :], d["dt_b"]), (w["skip"][:, :], d["skip"])]
        with nc.Block() as block:
            @block.sync
            def _(sp):
                for dst, src in loads:
                    sp.dma_start(dst, src).then_inc(w_loaded, 16)

            @block.scalar
            def _(act):
                act.wait_ge(w_loaded, 16 * len(loads))
                nc.scalar.activation(w["a"][:, :], w["a"][:, :], ACT.Exp).then_inc(a_exp, 1)
                act.wait_ge(a_exp, 1)
                nc.scalar.mul(w["a"][:, :], w["a"][:, :], -1.0)

            @block.tensor
            def _(pe):
                pe.wait_ge(w_loaded, 16 * len(loads))
                for h in range(2):
                    nc.tensor.matmul(pd[h][0:HALF, 0:DI], wx_t[:, h * HALF:(h + 1) * HALF], wdt[:, :], start=True, stop=True).then_inc(w_prod, 1)

            @block.vector
            def _(dve):
                dve.wait_ge(w_loaded, 16 * len(loads))
                for k in range(DCONV):
                    nc.vector.tensor_tensor(w["conv"][:, k, :], w_in[:, :], taps[:, k, :], ALU.mult)
                nc.vector.tensor_copy(w["spread"][:, :, :].rearrange("p q n -> p (q n)"), spread_f[:, :])
                for h in range(2):
                    dve.wait_ge(w_prod, h + 1)
                    nc.vector.tensor_copy(w["dt_bc"][:, h, 0:HALF], pd[h][0:HALF, 0:HALF])
                    nc.vector.tensor_copy(w["dt_bc"][:, h, HALF:P], wx[:, h, DR:])
                    nc.vector.tensor_copy(w["dt"][:, h, :], pd[h][0:HALF, HALF:DI])


def scan(nc, d, w):
    with ExitStack() as ctx:
        def sb(name, shape, dt=F32):
            return ctx.enter_context(nc.sbuf_tensor(name, shape, dt))

        def sem(name):
            return ctx.enter_context(nc.semaphore(name))

        def pair(name, make=None):
            return [(make or sem)(f"{name}{i}") for i in range(2)]

        NDA, NDB, NHR, NHC = 3, 2, 3, 4
        decay = [sb(f"decay{i}", [P, T]) for i in range(NDA)]
        drive = [sb(f"drive{i}", [P, T]) for i in range(NDB)]
        hring = sb("hring", [P, NHR * T + 1])
        hc = [sb(f"hc{i}", [P, T]) for i in range(NHC)]
        carry = sb("carry", [P, 2, UNITS])
        b_rep = pair("b_rep", lambda n: sb(n, [P, T]))
        c_rep = pair("c_rep", lambda n: sb(n, [P, T]))
        stack_dt = pair("stack_dt", lambda n: sb(n, [HALF, 3, T]))
        stack_u = pair("stack_u", lambda n: sb(n, [HALF, 3, T]))
        xn = pair("xn", lambda n: sb(n, [C, XN]))
        xa = pair("xa", lambda n: sb(n, [HALF, 2, T]))
        y_sb = pair("y_sb", lambda n: sb(n, [HALF, T]))
        dt3 = [sb(f"dt3_{i}", [HALF, T]) for i in range(3)]
        u3 = [sb(f"u3_{i}", [HALF, T]) for i in range(3)]
        soft = sb("soft", [HALF, T])
        ramp = sb("ramp", [HALF, T])
        bc = sb("bc", [P, T])

        dt_ps = [ctx.enter_context(nc.psum_tensor(f"dt_ps{i}", [P, SL], F32)) for i in range(2)]
        u_ps = [ctx.enter_context(nc.psum_tensor(f"u_ps{i}", [P, SL], F32)) for i in range(3)]
        y_ps = ctx.enter_context(nc.psum_tensor("y_ps", [P, 2 * SL], F32))
        prep_ps = ctx.enter_context(nc.psum_tensor("prep_ps", [P, SL], F32))

        zeroed = sem("zeroed")
        dt_spread = sem("dt_spread")
        u_spread = sem("u_spread")
        decay_ready = sem("decay_ready")
        drive_ready = sem("drive_ready")
        scanned = sem("scanned")
        carried = sem("carried")
        c_applied = sem("c_applied")
        summed = sem("summed")
        y_ready = sem("y_ready")
        y_stored = pair("y_stored")
        xn_in = pair("xn_in")
        prep_done = sem("prep_done")
        prep_out = sem("prep_out")
        silu_done = sem("silu_done")
        soft_step = sem("soft_step")
        dt_ready = sem("dt_ready")
        u_ready = sem("u_ready")
        split = sem("split")
        bc_stored = sem("bc_stored")
        b_in = pair("b_in")
        c_in = pair("c_in")
        stack_in = pair("stack_in")

        NPREP = 8
        STACKED = 16 * 18
        CONV_AT = (0, 2, 4, 6)
        DT_AT = ((9, 10), (14, 15))

        def group(n):
            return n // HU, n % HU // 3, n % 3

        def run(eng, front, back=None, prep=None, back_last=False):
            if prep:
                for m in range(UNITS):
                    prep(m, 0, 0, 0)
            for n in range(LEAD):
                front(n, n, 0, 0)
            with eng.Fori(0, ITERS) as it:
                for dr in range(2):
                    p = 2 * it + dr
                    nxt = (it + dr, 1 - dr)
                    for m in range(UNITS):
                        n = m + LEAD
                        where = (n, it, dr) if n < UNITS else (n - UNITS,) + nxt
                        if back and not back_last:
                            back(m, p, it, dr)
                        front(UNITS * p + n, *where)
                        if back and back_last:
                            back(m, p, it, dr)
                        if prep:
                            prep(m, p + 1, *nxt)
                    if back:
                        back(UNITS, p, it, dr)

        with nc.Block() as block:
            @block.sync
            def _(sp):
                def load_xn(buf, img, tok):
                    sp.dma_start(xn[buf][:, :], d["xn_scr"][img, :, bass.ds(tok, XN)]).then_inc(xn_in[buf], 16)

                def prep_loads(pn, it, dr):
                    sp.wait_ge(prep_out, NPREP * pn + 6)
                    sp.dma_start(d["bc_scr"][dr], bc[HALF:P, :]).then_inc(bc_stored, 16)
                    first = isinstance(pn, int)
                    if not first:
                        sp.wait_ge(c_applied, UNITS * (pn - 1))
                    sp.wait_ge(bc_stored, 16 * (pn + 1))
                    for dst, lo, s in ((b_rep, 0, b_in), (c_rep, DS, c_in)):
                        sp.dma_start(dst[dr][:, :], d["bc_scr"][dr][lo:lo + DS, :].partition_broadcast(GC)).then_inc(s[dr], 16)
                    for h in range(2):
                        if not first:
                            sp.wait_ge(u_spread, 2 * (UNITS * (pn - 1) + HU * (h + 1)))
                        for parts, dst, step in ((dt3, stack_dt, 2), (u3, stack_u, 4)):
                            sp.wait_ge(split, 4 * (2 * pn + h) + step)
                            for i in range(3):
                                for j in range(3):
                                    sp.dma_start(dst[h][32 * i:32 * i + 32, j, :], parts[i][32 * j:32 * j + 32, :]).then_inc(stack_in[h], 16)
                        yield h

                for buf in range(2):
                    load_xn(buf, 0, 0 if buf == 0 else (CHUNKS - 1) * T)
                for _ in prep_loads(0, 0, 0):
                    pass
                with sp.Fori(0, ITERS) as it:
                    for dr in range(2):
                        p = 2 * it + dr
                        after = (it + 1) % ITERS
                        img, img2 = it // CHUNKS, after // CHUNKS
                        tok, tok2 = (v % CHUNKS * T if dr == 0 else v % CHUNKS * -T + (CHUNKS - 1) * T for v in (it, after))
                        sp.wait_ge(prep_done, NPREP * p + 4)
                        load_xn(dr, img2, tok2)
                        for h in prep_loads(p + 1, it + dr, 1 - dr):
                            sp.wait_ge(y_ready, 2 * p + h + 1)
                            sp.dma_start(d["y_scr"][dr][img, h * HALF:(h + 1) * HALF, bass.ds(tok, T)],
                                         y_sb[h][:, :]).then_inc(y_stored[h], 16)
                for h in range(2):
                    sp.wait_ge(y_stored[h], 16 * 2 * ITERS)
                    sp.wait_ge(xn_in[h], 16 * (ITERS + 1))
                    sp.wait_ge(stack_in[h], STACKED * (2 * ITERS + 1))
                sp.wait_ge(b_in[0], 16 * (ITERS + 1))
                sp.wait_ge(c_in[0], 16 * (ITERS + 1))

            @block.tensor
            def _(pe):
                def spread(dst, stack, n, i):
                    h, q, j = group(n)
                    return nc.tensor.matmul(dst[:, :], w["spread"][:, q, :], upper(stack[h][:, j, i * SL:(i + 1) * SL]),
                                            start=True, stop=True)

                def front(u, n, it, dr):
                    if n % HU == 0:
                        pe.wait_ge(stack_in[n // HU], STACKED * (2 * it + dr + 1))
                    for i in range(2):
                        wait(pe, decay_ready, 2 * (u - 1) + i + 1, u)
                        spread(dt_ps[i], stack_dt, n, i).then_inc(dt_spread, 1)
                    for i in range(2):
                        wait(pe, drive_ready, 2 * u + i - 2, not isinstance(u, int) or 2 * u + i - 2 > 0)
                        spread(u_ps[(2 * n + i) % 3], stack_u, n, i).then_inc(u_spread, 1)

                def back(n, p, it, dr):
                    if n == UNITS:
                        return
                    h, q, j = group(n)
                    pe.wait_ge(c_applied, UNITS * p + n + 1)
                    if n % HU == 0:
                        pe.wait_ge(y_ready, 2 * p + h)
                    for i in range(2):
                        last = nc.tensor.matmul(y_ps[32 * j:32 * j + 32, i * SL:(i + 1) * SL], w["gather"][:, q, :],
                                                hc[n % NHC][:, i * SL:(i + 1) * SL], start=(q == 0), stop=(q == QN - 1))
                    last.then_inc(summed, 1)

                def prep(m, pn, it, dr):
                    if m in CONV_AT:
                        g = CONV_AT.index(m)
                        h, s = divmod(g, 2)
                        if g == 0:
                            pe.wait_ge(xn_in[dr], 16 * (it + 1))
                        wait(pe, prep_out, NPREP * pn + g, not isinstance(pn, int) or g > 0)
                        for k in range(DCONV):
                            at = s * SL + (k if dr == 0 else 2 * HALO - k)
                            last = nc.tensor.matmul(prep_ps[0:HALF, :], w["conv"][:, k, h * HALF:(h + 1) * HALF],
                                                    xn[dr][:, at:at + SL], start=(k == 0), stop=(k == DCONV - 1))
                        last.then_inc(prep_done, 1)
                    for h in range(2):
                        if m in DT_AT[h]:
                            s = DT_AT[h].index(m)
                            pe.wait_ge(silu_done, pn + 1)
                            pe.wait_ge(prep_out, NPREP * pn + 4 + 2 * h + s)
                            mat = w["dt"] if h else w["dt_bc"]
                            rows = HALF if h else P
                            for k in range(2):
                                last = nc.tensor.matmul(prep_ps[0:rows, :], mat[:, k, :], xa[dr][:, k, s * SL:(s + 1) * SL],
                                                        start=(k == 0), stop=(k == 1))
                            last.then_inc(prep_done, 1)

                run(pe, front, back, prep, back_last=True)

            @block.scalar
            def _(act):
                def front(u, n, it, dr):
                    h, q, j = group(n)
                    col = h * HU + j * QN + q
                    wait(act, scanned, u - NDA + 1, not isinstance(u, int) or u >= NDA)
                    for i in range(2):
                        act.wait_ge(dt_spread, 2 * u + i + 1)
                        nc.scalar.activation(decay[n % NDA][:, i * SL:(i + 1) * SL], dt_ps[i][:, :], ACT.Exp,
                                             scale=w["a"][:, col:col + 1]).then_inc(decay_ready, 1)
                    if isinstance(u, int) and u < NDA:
                        return
                    v, nv = u - NDA, (n - NDA) % UNITS
                    if n >= NDA:
                        drv, itv = dr, it
                    else:
                        drv, itv = 1 - dr, it if dr == 1 else it - 1
                    col = (nv % NHR) * T + (T - 1 if drv == 0 else 0)
                    at = col + (itv % CHUNKS) // (CHUNKS - 1) * (NHR * T - col)
                    nc.scalar.copy(carry[:, drv, nv:nv + 1], hring[:, bass.ds(at, 1)]).then_inc(carried, 1)

                def prep(m, pn, it, dr):
                    if m - 1 in CONV_AT:
                        g = CONV_AT.index(m - 1)
                        h, s = divmod(g, 2)
                        if g == 0:
                            wait(act, y_ready, 2 * (pn - 1), pn)
                        act.wait_ge(prep_done, NPREP * pn + g + 1)
                        nc.scalar.activation(xa[dr][:, h, s * SL:(s + 1) * SL], prep_ps[0:HALF, :], ACT.Identity,
                                             bias=w["conv_b"][:, h:h + 1]).then_inc(prep_out, 1)
                        if g == 3:
                            act.wait_ge(prep_out, NPREP * pn + 4)
                            nc.scalar.activation(xa[dr][:, :, :], xa[dr][:, :, :], ACT.Silu).then_inc(silu_done, 1)
                    for h in range(2):
                        if m - 1 in DT_AT[h]:
                            s = DT_AT[h].index(m - 1)
                            act.wait_ge(prep_done, NPREP * pn + 4 + 2 * h + s + 1)
                            if s == 0:
                                wait(act, dt_ready, 2 * pn + h, not isinstance(pn, int) or h > 0)
                            sl = slice(s * SL, (s + 1) * SL)
                            if h == 0:
                                if s == 0:
                                    wait(act, bc_stored, 16 * pn, pn)
                                nc.scalar.copy(bc[HALF:P, sl], prep_ps[HALF:P, :])
                            nc.scalar.activation(soft[:, sl], prep_ps[0:HALF, :], ACT.Abs, bias=w["dt_b"][:, h:h + 1])
                            nc.scalar.activation(ramp[:, sl], prep_ps[0:HALF, :], ACT.Relu, bias=w["dt_b"][:, h:h + 1]).then_inc(prep_out, 1)
                            if s == 1:
                                act.wait_ge(prep_out, NPREP * pn + 4 + 2 * h + 2)
                                nc.scalar.activation(soft[:, :], soft[:, :], ACT.Exp, scale=-1.0).then_inc(soft_step, 1)
                                act.wait_ge(soft_step, 2 * (2 * pn + h) + 1)
                                nc.scalar.activation(soft[:, :], soft[:, :], ACT.Ln, bias=1.0).then_inc(soft_step, 1)

                act.wait_ge(zeroed, 1)
                run(act, front, None, prep)

            @block.vector
            def _(dve):
                nc.vector.memset(hring[:, NHR * T:], 0.0)
                nc.vector.memset(carry[:, :, :], 0.0).then_inc(zeroed, 1)
                dve.wait_ge(zeroed, 1)

                def front(u, n, it, dr):
                    if n == 0:
                        dve.wait_ge(b_in[dr], 16 * (it + 1))
                    wait(dve, scanned, u - NDB + 1, not isinstance(u, int) or u >= NDB)
                    for i in range(2):
                        dve.wait_ge(u_spread, 2 * u + i + 1)
                        sl = slice(i * SL, (i + 1) * SL)
                        nc.vector.tensor_tensor(drive[n % NDB][:, sl], u_ps[(2 * n + i) % 3][:, :], b_rep[dr][:, sl],
                                                ALU.mult).then_inc(drive_ready, 1)
                    if isinstance(u, int) and u == 0:
                        return
                    v, nv = u - 1, (n - 1) % UNITS
                    drv = dr if n >= 1 else 1 - dr
                    dve.wait_ge(decay_ready, 2 * v + 2)
                    dve.wait_ge(drive_ready, 2 * v + 2)
                    wait(dve, c_applied, v - NHR + 1, not isinstance(v, int) or v >= NHR)
                    wait(dve, carried, v - NHR + 1, not isinstance(v, int) or v >= NHR)
                    r = nv % NHR
                    step = 1 if drv == 0 else -1
                    nc.vector.tensor_tensor_scan(hring[:, r * T:(r + 1) * T][:, ::step], decay[nv % NDA][:, ::step],
                                                 drive[nv % NDB][:, ::step], carry[:, drv, nv:nv + 1],
                                                 ALU.mult, ALU.add).then_inc(scanned, 1)

                def back(n, p, it, dr):
                    if n == 0 or n % HU:
                        return
                    h = n // HU - 1
                    dve.wait_ge(summed, UNITS * p + n)
                    dve.wait_ge(y_stored[h], 16 * p)
                    nc.vector.scalar_tensor_tensor(y_sb[h][:, :], xa[dr][:, h, :], w["skip"][:, h:h + 1], y_ps[0:HALF, :],
                                                   ALU.mult, ALU.add).then_inc(y_ready, 1)

                def prep(m, pn, it, dr):
                    for h in range(2):
                        at = DT_AT[h][1] + 3
                        done = 4 * (2 * pn + h)
                        for i, (parts, ready) in enumerate(((dt3, dt_ready), (u3, u_ready))):
                            if m == at + i + 1:
                                dve.wait_ge(ready, 2 * pn + h + 1)
                                nc.vector.tensor_tensor(parts[1][:, :], parts[0][:, :], upper(parts[0][:, :]), ALU.subtract).then_inc(split, 1)
                                dve.wait_ge(split, done + 2 * i + 1)
                                nc.vector.tensor_tensor(parts[2][:, :], parts[1][:, :], upper(parts[1][:, :]), ALU.subtract).then_inc(split, 1)

                run(dve, front, back, prep)

            @block.gpsimd
            def _(pool):
                def front(u, n, it, dr):
                    if isinstance(u, int) and u == 0:
                        return
                    v, nv = u - 1, (n - 1) % UNITS
                    drv = dr if n >= 1 else 1 - dr
                    if nv == 0:
                        pool.wait_ge(c_in[dr], 16 * (it + 1))
                    pool.wait_ge(scanned, v + 1)
                    wait(pool, summed, v - NHC + 1, not isinstance(v, int) or v >= NHC)
                    r = nv % NHR
                    nc.gpsimd.tensor_tensor(hc[nv % NHC][:, :], hring[:, r * T:(r + 1) * T], c_rep[drv][:, :],
                                            ALU.mult).then_inc(c_applied, 1)

                def prep(m, pn, it, dr):
                    for h in range(2):
                        if m == DT_AT[h][1] + 3:
                            pool.wait_ge(soft_step, 2 * (2 * pn + h) + 2)
                            wait(pool, stack_in[1 - h], STACKED * (pn + h), not isinstance(pn, int) or h > 0)
                            nc.gpsimd.tensor_tensor(dt3[0][:, :], soft[:, :], ramp[:, :], ALU.add).then_inc(dt_ready, 1)
                            pool.wait_ge(dt_ready, 2 * pn + h + 1)
                            pool.wait_ge(silu_done, pn + 1)
                            nc.gpsimd.tensor_tensor(u3[0][:, :], dt3[0][:, :], xa[dr][:, h, :], ALU.mult).then_inc(u_ready, 1)

                run(pool, front, None, prep)


def output(nc, d, w):
    NS = L // SL
    with ExitStack() as ctx:
        def sb(name, shape, dt=F32):
            return ctx.enter_context(nc.sbuf_tensor(name, shape, dt))

        def sem(name):
            return ctx.enter_context(nc.semaphore(name))

        R = 4
        yf = sb("yf", [HALF, R, 2, SL])
        yb = sb("yb", [HALF, R, 2, SL])
        xz = sb("xz", [C, R, SL])
        ys = sb("ys", [HALF, R, 2, SL])
        sz = sb("sz", [HALF, R, 2, SL])
        yg = sb("yg", [HALF, R, 2, SL])
        res = sb("res", [C, R, SL])
        pz = [ctx.enter_context(nc.psum_tensor(f"pz{i}", [P, 2 * SL], F32)) for i in range(2)]
        po = [ctx.enter_context(nc.psum_tensor(f"po{i}", [P, SL], F32)) for i in range(2)]
        o_loaded = [sem(f"o_loaded{i}") for i in range(R)]
        o_stored = [sem(f"o_stored{i}") for i in range(R)]
        y_sum = sem("y_sum")
        z_made = sem("z_made")
        z_silu = sem("z_silu")
        gated = sem("gated")
        projected = sem("projected")
        res_ready = sem("res_ready")
        with nc.Block() as block:
            @block.sync
            def _(sp):
                with sp.Fori(0, B) as b:
                    for s in range(NS):
                        r = s % R
                        if s >= R:
                            sp.wait_ge(y_sum, NS * b + s - R + 1)
                            sp.wait_ge(z_made, NS * b + s - R + 1)
                        elif s == 0:
                            sp.wait_ge(y_sum, NS * b)
                            sp.wait_ge(z_made, NS * b)
                        sl = slice(s * SL, (s + 1) * SL)
                        for t, src in ((yf, d["y_scr"][0]), (yb, d["y_scr"][1])):
                            sp.dma_start(t[:, r, :, :], src[b, :, sl].rearrange("(h c) t -> c h t", h=2)).then_inc(o_loaded[r], 16)
                        sp.dma_start(xz[:, r, :], d["xn_scr"][b, :, HALO + s * SL:HALO + (s + 1) * SL]).then_inc(o_loaded[r], 16)
                for r in range(R):
                    sp.wait_ge(o_stored[r], 16 * (B * NS // R))

            @block.gpsimd
            def _(pool):
                with pool.Fori(0, B) as b:
                    for s in range(NS):
                        r = s % R
                        pool.wait_ge(o_loaded[r], 48 * (NS // R * b + s // R + 1))
                        if s >= R:
                            pool.wait_ge(gated, NS * b + s - R + 1)
                        elif s == 0:
                            pool.wait_ge(gated, NS * b)
                        nc.gpsimd.tensor_tensor(ys[:, r, :, :], yf[:, r, :, :], yb[:, r, :, :], ALU.add).then_inc(y_sum, 1)

            @block.tensor
            def _(pe):
                with pe.Fori(0, B) as b:
                    pe.wait_ge(z_silu, NS * b)
                    pe.wait_ge(res_ready, NS * b)
                    for s in range(NS + 1):
                        if s < NS:
                            pe.wait_ge(o_loaded[s % R], 48 * (NS // R * b + s // R + 1))
                            wait(pe, z_silu, NS * b + s - 1, s >= 2)
                            for h in range(2):
                                last = nc.tensor.matmul(pz[s % 2][0:HALF, h * SL:(h + 1) * SL], w["z"][:, h * HALF:(h + 1) * HALF],
                                                        xz[:, s % R, :], start=True, stop=True)
                            last.then_inc(z_made, 1)
                        if s >= 1:
                            v = s - 1
                            pe.wait_ge(gated, NS * b + v + 1)
                            wait(pe, res_ready, NS * b + v - 1, v >= 2)
                            for h in range(2):
                                last = nc.tensor.matmul(po[v % 2][0:C, :], w["out"][:, h, :], yg[:, v % R, h, :], start=(h == 0), stop=(h == 1))
                            last.then_inc(projected, 1)

            @block.scalar
            def _(act):
                with act.Fori(0, B) as b:
                    act.wait_ge(gated, NS * b)
                    for s in range(NS + 2):
                        if s < NS:
                            act.wait_ge(z_made, NS * b + s + 1)
                            wait(act, gated, NS * b + s - R + 1, s >= R)
                            nc.scalar.activation(sz[:, s % R, :, :].rearrange("p h t -> p (h t)"), pz[s % 2][0:HALF, :], ACT.Silu).then_inc(z_silu, 1)
                        if s >= 2:
                            v = s - 2
                            r = v % R
                            act.wait_ge(projected, NS * b + v + 1)
                            act.wait_ge(o_stored[r], 16 * (NS // R * b + v // R))
                            nc.scalar.copy(res[:, r, :], po[v % 2][0:C, :]).then_inc(res_ready, 1)
                            act.wait_ge(res_ready, NS * b + v + 1)
                            act.dma_start(d["out"][b, :, v * SL:(v + 1) * SL], res[:, r, :]).then_inc(o_stored[r], 16)

            @block.vector
            def _(dve):
                with dve.Fori(0, B) as b:
                    dve.wait_ge(projected, NS * b)
                    for s in range(NS):
                        r = s % R
                        dve.wait_ge(y_sum, NS * b + s + 1)
                        dve.wait_ge(z_silu, NS * b + s + 1)
                        wait(dve, projected, NS * b + s - R + 1, s >= R)
                        nc.vector.tensor_tensor(yg[:, r, :, :], ys[:, r, :, :], sz[:, r, :, :], ALU.mult).then_inc(gated, 1)


def mixer_weights(nc, ctx):
    shapes = {"conv": ([HALF, DCONV, DI], F32), "dt_bc": ([HALF, 2, P], F32), "dt": ([HALF, 2, HALF], F32),
              "z": ([C, DI], F32), "out": ([HALF, 2, C], F32), "a": ([P, UNITS], F32),
              "spread": ([HALF, QN, P], BF16), "gather": ([P, QN, 32], F32),
              "conv_b": ([HALF, 2], F32), "dt_b": ([HALF, 2], F32), "skip": ([HALF, 2], F32)}
    return {n: ctx.enter_context(nc.sbuf_tensor("w_" + n, s, t)) for n, (s, t) in shapes.items()}


def vision_mixer_kernel(nc, d):
    d["act_scr"] = nc.dram_tensor("act_scr", [B, C, L], F32, kind="Internal").ap()
    d["xn_scr"] = nc.dram_tensor("xn_scr", [B, C, L + 2 * HALO], F32, kind="Internal").ap()
    d["y_scr"] = [nc.dram_tensor(f"y_scr{i}", [B, DI, L], F32, kind="Internal").ap() for i in range(2)]
    d["bc_scr"] = [nc.dram_tensor(f"bc_scr{i}", [2 * DS, T], F32, kind="Internal").ap() for i in range(2)]
    with nc.sbuf_tensor("gate", [C, B], F32) as gate:
        with nc.sbuf_tensor("hs", [P, C * B * XH], F32) as hs:
            convolution(nc, d, hs)
            pointwise(nc, d, hs, gate)
        normalise(nc, d, gate)
    with ExitStack() as ctx:
        w = mixer_weights(nc, ctx)
        weights(nc, d, w)
        scan(nc, d, w)
        output(nc, d, w)


def layout(inputs):
    import numpy as np
    f = {k: np.ascontiguousarray(v) for k, v in inputs.items()}
    x = f["x"]
    d = {}
    d["x_cols"] = x.reshape(B, C, H, XH, 2).transpose(4, 2, 1, 0, 3).reshape(P, C, B, XH)
    d["x_tok"] = x.reshape(B, C, L)
    fp = np.pad(f["L0_conv_plk_filter"].reshape(C, K, K), ((0, 0), (0, 0), (1, 1)))
    cols = np.empty((2, K, C, SHIFTS, 2), np.float32)
    for pi in range(2):
        for po in range(2):
            for s in range(SHIFTS):
                cols[pi, :, :, s, po] = fp[:, :, 2 * s + pi - po + 1].T
    d["filter_cols"] = cols.reshape(FROWS, C * FCOLS)
    band = np.zeros((3, 2, K, 2, 2 * H - 1), np.float32)
    for pi in range(2):
        for dy in range(K):
            band[:, pi, dy, pi, H - 1 + dy - PAD] = 1.0
    d["band"] = band.reshape(3 * FROWS, -1)
    m = np.zeros((3, FROWS, 2), np.float32)
    m[1:, :, 0] = -1.0
    m[2:, :, 1] = -1.0
    d["split_masks"] = m.reshape(3 * FROWS, 2)
    for n in ("gamma", "beta", "mean", "var"):
        d["bn1_" + n] = f["L0_conv_bn1_" + n]
        d["bn2_" + n] = f["L0_conv_bn2_" + n]
    d["ident"] = np.eye(P, dtype=np.float32)
    d["pw_t"] = f["L0_conv_pw_weight"].T
    d["se_w1_t"] = f["L0_conv_se_w1"].T
    d["se_w2_t"] = f["L0_conv_se_w2"].T
    d["se_b1"] = f["L0_conv_se_b1"]
    d["se_b2"] = f["L0_conv_se_b2"]
    d["gamma"] = f["L0_conv_gamma"]
    d["averager"] = np.full((C, C), 1.0 / C, np.float32)
    d["ln_g"] = f["L1_conv_ln_g"]
    d["ln_b"] = f["L1_conv_ln_b"]
    d["w_in"] = f["L1_conv_W_in"]
    d["conv_taps"] = f["L1_conv_conv_w"].T.reshape(-1)
    d["w_x"] = f["L1_conv_W_xproj"].reshape(2, HALF, -1).transpose(1, 0, 2)
    d["w_x_t"] = f["L1_conv_W_xproj"][:, :DR].T
    d["w_dt"] = f["L1_conv_W_dt"]
    d["a_log"] = f["L1_conv_A_log"].reshape(UNITS, P).T
    d["w_out"] = f["L1_conv_W_out"].reshape(2, HALF, C).transpose(1, 0, 2)
    d["conv_b"] = f["L1_conv_conv_b"].reshape(2, HALF).T
    d["dt_b"] = f["L1_conv_b_dt"].reshape(2, HALF).T
    d["skip"] = f["L1_conv_D"].reshape(2, HALF).T
    spread = np.zeros((3, 32, QN, GC, DS), np.float32)
    gather = np.zeros((GC, DS, QN, 32), np.float32)
    for r in range(32):
        spread[:, r, r // GC, r % GC, :] = 1.0
        gather[r % GC, :, r // GC, r] = 1.0
    d["spread"] = spread.reshape(HALF, QN * P)
    d["gather"] = gather.reshape(P, QN * 32)
    return {k: np.ascontiguousarray(v) for k, v in d.items()}


def kernel(**inputs):
    import numpy as np
    import concourse.bacc as bacc
    from concourse.bass_utils import run_bass_kernel_spmd

    nc = bacc.Bacc("TRN2", target_bir_lowering=False, num_devices=1)
    arrays, drams = {}, {}
    for name, a in layout({k: np.asarray(v) for k, v in inputs.items()}).items():
        arrays["in_" + name] = a
        drams[name] = nc.dram_tensor("in_" + name, a.shape, mybir.dt.from_np(a.dtype), kind="ExternalInput").ap()
    drams["out"] = nc.dram_tensor("out", (B, C, L), F32, kind="ExternalOutput").ap()
    vision_mixer_kernel(nc, drams)
    result = run_bass_kernel_spmd(nc, [arrays], core_ids=[0])
    return result.results[0]["out"].reshape(B, C, H, W)
```

```python
from contextlib import ExitStack

import concourse.bass as bass
from concourse import mybir

F32 = mybir.dt.float32
BF16 = mybir.dt.bfloat16
ALU = mybir.AluOpType
ACT = mybir.ActivationFunctionType
AX_X = mybir.AxisListType.X

P = 128
B, C, H, W = 8, 96, 64, 64
L = H * W
BN_EPS = 1e-5
LN_EPS = 1e-5

K = 17
PAD = K // 2
XH = W // 2
SHIFTS = PAD + 1
NEAR = PAD // 2
XP = XH + 2 * NEAR
CB = 4
BATCHES = C // CB
FCOLS = SHIFTS * 2
FROWS = 2 * K
YG = 4
NYG = H // YG

DI = 192
HALF = DI // 2
DS = 16
DR = 6
DCONV = 4
T = 1024
SL = 512
CHUNKS = L // T
HALO = DCONV - 1
XN = T + 2 * HALO
GC = P // DS
UNITS = DI // GC
HU = UNITS // 2
QN = 32 // GC
ITERS = B * CHUNKS
EXP_LN = 6
LEAD = 6


def upper(ap):
    return ap.bitcast(BF16)[:, 1::2]



def wait(eng, sem, count, when=True):
    if when is True or not isinstance(when, (bool, int)) or when:
        eng.wait_ge(sem, count)


def convolution(nc, d, hs):
    with ExitStack() as ctx:
        def sb(name, shape, dt=F32):
            return ctx.enter_context(nc.sbuf_tensor(name, shape, dt))

        def sem(name):
            return ctx.enter_context(nc.semaphore(name))

        filt = sb("filt", [3 * FROWS, (C + CB) * FCOLS])
        filt_tmp = hs[0:3 * FROWS, 0:C * FCOLS]
        masks = sb("masks", [3 * FROWS, 2])
        band_f = sb("band_f", [3 * FROWS, 2 * (2 * H - 1)])
        band = sb("band", [3 * FROWS, 2, 2 * H - 1], BF16)
        bands = sb("bands", [3 * FROWS, H, P], BF16)
        toep = [sb(f"toep{i}", [P, CB * FCOLS, H]) for i in range(2)]
        xraw = [sb(f"xraw{i}", [P, CB, B, XH]) for i in range(2)]
        xpad = [sb(f"xpad{i}", [P, CB, B, XP]) for i in range(2)]
        bnp = sb("bnp", [P, 4, C])
        bnt = sb("bnt", [P, 3, C])
        scale = sb("scale", [P, C])
        shift = sb("shift", [P, C])
        eps = sb("eps", [P, 1])
        pw = [ctx.enter_context(nc.psum_tensor(f"pw{i}", [P, SL], F32)) for i in range(2)]
        pc = [ctx.enter_context(nc.psum_tensor(f"pc{i}", [P, SL], F32)) for i in range(CB)]

        const_in = sem("const_in")
        x_in = [sem(f"x_in{i}") for i in range(2)]
        eps_set = sem("eps_set")
        bn_sqrt = sem("bn_sqrt")
        bn_dve = sem("bn_dve")
        filt_step = sem("filt_step")
        band_ready = sem("band_ready")
        pads_zero = sem("pads_zero")
        x_ready = sem("x_ready")
        w_ready = sem("w_ready")
        w_evac = [sem(f"w_evac{i}") for i in range(2)]
        conv_done = [sem(f"conv_done{i}") for i in range(2)]
        h_evac = [sem(f"h_evac{i}") for i in range(CB)]

        xk = d["x_cols"]
        NCONST = 3 + 3 + 4
        after = [range(NYG // CB * i, NYG // CB * (i + 1)) for i in range(CB)]

        with nc.Block() as block:
            @block.sync
            def _(sp):
                for i in range(2):
                    sp.dma_start(xraw[i][:, :, :, :], xk[:, i * CB:(i + 1) * CB, :, :]).then_inc(x_in[i], 16)
                for i in range(3):
                    sp.dma_start(filt[i * FROWS:(i + 1) * FROWS, 0:C * FCOLS], d["filter_cols"]).then_inc(const_in, 16)
                sp.dma_start(band_f[:, :], d["band"]).then_inc(const_in, 16)
                sp.dma_start(masks[:, :], d["split_masks"]).then_inc(const_in, 16)
                for i, name in enumerate(("gamma", "beta", "mean", "var")):
                    sp.dma_start(bnp[:, i, :], d["bn1_" + name].partition_broadcast(P)).then_inc(const_in, 16)
                with sp.Fori(0, BATCHES // 2) as i:
                    for par in range(2):
                        ch = (2 * i + par + 2) % BATCHES * CB
                        sp.wait_ge(x_ready, 2 * i + par + 1)
                        sp.dma_start(xraw[par][:, :, :, :], xk[:, bass.ds(ch, CB), :, :]).then_inc(x_in[par], 16)
                for i in range(2):
                    sp.wait_ge(x_in[i], 16 * (BATCHES // 2 + 1))

            @block.gpsimd
            def _(pool):
                for i in range(2):
                    nc.gpsimd.memset(xpad[i][:, :, :, 0:NEAR], 0.0)
                    last = nc.gpsimd.memset(xpad[i][:, :, :, NEAR + XH:XP], 0.0)
                last.then_inc(pads_zero, 1)

            def evacuate_weights(eng, copy, s, buf, bank, yg, batches_before):
                if batches_before is not None:
                    eng.wait_ge(conv_done[buf], CB * batches_before)
                eng.wait_ge(w_ready, NYG * s + yg + 1)
                src = pw[bank][:, 0:YG * CB * FCOLS].rearrange("p (y n) -> p n y", y=YG)
                copy(toep[buf][:, :, yg * YG:(yg + 1) * YG], src).then_inc(w_evac[bank], 1)

            def evacuate_conv(eng, copy, i, par, c):
                s = 2 * i + par
                eng.wait_ge(conv_done[par], CB * i + c + 1)
                copy(hs[:, bass.ds((CB * s + c) * B * XH, B * XH)], pc[c][:, 0:B * XH]).then_inc(h_evac[c], 1)

            def evacuations(eng, copy, mine, norm=None):
                for yg in range(mine, NYG, 2):
                    evacuate_weights(eng, copy, 0, 0, mine, yg, None)
                with eng.Fori(0, BATCHES // 2) as i:
                    for par in range(2):
                        s = 2 * i + par
                        for c in range(CB):
                            if c % 2 == mine:
                                evacuate_conv(eng, copy, i, par, c)
                            for yg in after[c]:
                                if yg % 2 == mine:
                                    evacuate_weights(eng, copy, s + 1, 1 - par, mine, yg, i + par)
                            if norm and c == 1:
                                norm(i, par)

            @block.scalar
            def _(act):
                act.wait_ge(const_in, 16 * (NCONST - 1))
                act.wait_ge(eps_set, 1)
                nc.scalar.activation(bnt[:, 0, :], bnp[:, 3, :], ACT.Sqrt, bias=eps[:, 0:1]).then_inc(bn_sqrt, 1)
                evacuations(act, nc.scalar.copy, 0)

            @block.vector
            def _(dve):
                nc.vector.memset(filt[:, C * FCOLS:], 0.0)
                nc.vector.memset(eps[:, :], BN_EPS).then_inc(eps_set, 1)
                dve.wait_ge(const_in, 16 * (NCONST - 1))
                nc.vector.tensor_copy(band[:, :, :].rearrange("p a b -> p (a b)"), band_f[:, :]).then_inc(band_ready, 1)
                dve.wait_ge(band_ready, 1)
                for y in range(H):
                    last = nc.vector.tensor_copy(bands[:, y, :].rearrange("p (a b) -> p a b", a=2), band[:, :, H - 1 - y:2 * H - 1 - y])
                last.then_inc(band_ready, 1)
                f = filt[:, 0:C * FCOLS]
                nc.vector.scalar_tensor_tensor(filt_tmp, upper(f), masks[:, 0:1], f, ALU.mult, ALU.add).then_inc(filt_step, 1)
                dve.wait_ge(filt_step, 1)
                nc.vector.scalar_tensor_tensor(f, upper(filt_tmp), masks[:, 1:2], filt_tmp, ALU.mult, ALU.add).then_inc(filt_step, 1)
                dve.wait_ge(bn_sqrt, 1)
                nc.vector.reciprocal(bnt[:, 1, :], bnt[:, 0, :]).then_inc(bn_dve, 1)
                dve.wait_ge(bn_dve, 1)
                nc.vector.tensor_tensor(scale[:, :], bnt[:, 1, :], bnp[:, 0, :], ALU.mult).then_inc(bn_dve, 1)
                dve.wait_ge(bn_dve, 2)
                nc.vector.tensor_tensor(bnt[:, 2, :], scale[:, :], bnp[:, 2, :], ALU.mult).then_inc(bn_dve, 1)
                dve.wait_ge(bn_dve, 3)
                nc.vector.tensor_tensor(shift[:, :], bnp[:, 1, :], bnt[:, 2, :], ALU.subtract).then_inc(bn_dve, 2)
                dve.wait_ge(filt_step, 2)
                dve.wait_ge(bn_dve, 5)
                dve.wait_ge(pads_zero, 1)

                def batch_norm(s, buf, loads):
                    dve.wait_ge(x_in[buf], 16 * loads)
                    for c in range(CB):
                        at = s * CB + c
                        last = nc.vector.tensor_scalar(xpad[buf][:, c, :, NEAR:NEAR + XH], xraw[buf][:, c, :, :],
                                                       scale[:, bass.ds(at, 1)], shift[:, bass.ds(at, 1)], ALU.mult, ALU.add)
                    last.then_inc(x_ready, 1)

                def next_norm(i, par):
                    wait(dve, conv_done[1 - par], CB * (i + par), True)
                    batch_norm((2 * i + par + 1) % BATCHES, 1 - par, i + par + 1)

                batch_norm(0, 0, 1)
                evacuations(dve, nc.vector.tensor_copy, 1, next_norm)

            @block.tensor
            def _(pe):
                pe.wait_ge(filt_step, 2)
                pe.wait_ge(band_ready, 2)

                def weights(s, yg):
                    bank = yg % 2
                    pe.wait_ge(w_evac[bank], (NYG // 2) * s + yg // 2)
                    for r in range(YG):
                        y = yg * YG + r
                        last = nc.tensor.matmul(pw[bank][:, r * CB * FCOLS:(r + 1) * CB * FCOLS],
                                                bands[:, y, :],
                                                filt[:, bass.ds(s * (CB * FCOLS), CB * FCOLS)].bitcast(BF16)[:, 1::2],
                                                start=True, stop=True, skip_group_check=True)
                    last.then_inc(w_ready, 1)

                for yg in range(NYG):
                    weights(0, yg)
                pe.wait_ge(pads_zero, 1)
                with pe.Fori(0, BATCHES // 2) as i:
                    for par in range(2):
                        s = 2 * i + par
                        pe.wait_ge(x_ready, s + 1)
                        for bank in range(2):
                            pe.wait_ge(w_evac[bank], (NYG // 2) * (s + 1))
                        for c in range(CB):
                            pe.wait_ge(h_evac[c], s)
                            for k in range(SHIFTS):
                                n0 = (c * SHIFTS + k) * 2
                                last = nc.tensor.matmul(pc[c][:, 0:B * XH].rearrange("p (b x) -> p b x", b=B),
                                                        toep[par][:, n0:n0 + 2, :].rearrange("p a y -> p (a y)"),
                                                        xpad[par][:, c, :, k:k + XH],
                                                        start=(k == 0), stop=(k == SHIFTS - 1))
                            last.then_inc(conv_done[par], 1)
                            for yg in after[c]:
                                weights(s + 1, yg)


def pointwise(nc, d, hs, gate):
    with ExitStack() as ctx:
        def sb(name, shape, dt=F32):
            return ctx.enter_context(nc.sbuf_tensor(name, shape, dt))

        def sem(name):
            return ctx.enter_context(nc.semaphore(name))

        HID = 32
        GROUPS = B * XH // 4
        GPB = GROUPS // B
        ident = sb("ident", [P, P])
        wpw = sb("wpw", [C, C])
        se1 = sb("se1", [C, HID])
        se2 = sb("se2", [HID, C])
        b1 = sb("b1", [HID, 1])
        b2 = sb("b2", [C, 1])
        gam = sb("gam", [C, 1])
        bn = sb("bn", [C, 4])
        bt = sb("bt", [C, 5])
        ht = [sb(f"ht{i}", [C, SL]) for i in range(2)]
        act_out = [sb(f"act_out{i}", [C, H, W]) for i in range(2)]
        sums = sb("sums", [C, GROUPS])
        mean = sb("mean", [C, B])
        hid = sb("hid", [HID, B])
        sig = sb("sig", [C, B])
        pt = [ctx.enter_context(nc.psum_tensor(f"pt{i}", [P, SL], F32)) for i in range(2)]
        pp = [ctx.enter_context(nc.psum_tensor(f"pp{i}", [P, SL], F32)) for i in range(2)]
        ps = [ctx.enter_context(nc.psum_tensor(f"ps{i}", [P, SL], F32)) for i in range(2)]

        p_in = sem("p_in")
        bn_s = sem("bn_s")
        bn_v = sem("bn_v")
        turned = sem("turned")
        t_evac = sem("t_evac")
        mixed = sem("mixed")
        gelu_done = sem("gelu_done")
        g_out = [sem(f"g_out{i}") for i in range(2)]
        se_mean = sem("se_mean")
        se_hid = sem("se_hid")
        se_relu = sem("se_relu")
        se_out = sem("se_out")
        se_sig = sem("se_sig")
        loads = [(ident[:, :], d["ident"]), (wpw[:, :], d["pw_t"]), (se1[:, :], d["se_w1_t"]), (se2[:, :], d["se_w2_t"]),
                 (b1[:, :], d["se_b1"].unsqueeze(1)), (b2[:, :], d["se_b2"].unsqueeze(1)),
                 (gam[:, :], d["gamma"].partition_broadcast(C))]
        loads += [(bn[:, i:i + 1], d["bn2_" + n].unsqueeze(1)) for i, n in enumerate(("gamma", "beta", "mean", "var"))]

        with nc.Block() as block:
            @block.sync
            def _(sp):
                for dst, src in loads:
                    sp.dma_start(dst, src).then_inc(p_in, 16)
                for b in range(B):
                    sp.wait_ge(gelu_done, GPB * (b + 1))
                    sp.dma_start(d["act_scr"][b], act_out[b % 2][:, :, :].rearrange("c y x -> c (y x)")).then_inc(g_out[b % 2], 16)
                for i in range(2):
                    sp.wait_ge(g_out[i], 16 * (B // 2))

            @block.tensor
            def _(pe):
                pe.wait_ge(p_in, 16 * len(loads))

                def mix(g):
                    pe.wait_ge(t_evac, g + 1)
                    if g >= 2:
                        pe.wait_ge(gelu_done, g - 1)
                    nc.tensor.matmul(pp[g % 2][0:C, :], wpw[:, :], ht[g % 2][:, :], start=True, stop=True).then_inc(mixed, 1)

                for g in range(GROUPS):
                    if g >= 2:
                        pe.wait_ge(t_evac, g - 1)
                    for r in range(4):
                        last = nc.tensor.transpose(pt[g % 2][0:C, r * P:(r + 1) * P],
                                                   hs[:, :].rearrange("p (c n) -> p c n", c=C)[:, :, 4 * g + r], ident[:, :])
                    last.then_inc(turned, 1)
                    if g >= 1:
                        mix(g - 1)
                mix(GROUPS - 1)
                pe.wait_ge(se_mean, 2)
                nc.tensor.matmul(ps[0][0:HID, 0:B], se1[:, :], mean[:, :], start=True, stop=True).then_inc(se_hid, 1)
                pe.wait_ge(se_relu, 1)
                nc.tensor.matmul(ps[1][0:C, 0:B], se2[:, :], hid[:, :], start=True, stop=True).then_inc(se_out, 1)

            @block.vector
            def _(dve):
                nc.vector.memset(bt[:, 4:5], BN_EPS).then_inc(bn_s, 1)
                dve.wait_ge(bn_s, 2)
                nc.vector.reciprocal(bt[:, 1:2], bt[:, 0:1]).then_inc(bn_v, 1)
                dve.wait_ge(bn_v, 1)
                nc.vector.tensor_tensor(bt[:, 2:3], bt[:, 1:2], bn[:, 0:1], ALU.mult).then_inc(bn_v, 1)
                dve.wait_ge(bn_v, 2)
                nc.vector.tensor_tensor(bt[:, 1:2], bt[:, 2:3], bn[:, 2:3], ALU.mult).then_inc(bn_v, 1)
                dve.wait_ge(bn_v, 3)
                nc.vector.tensor_tensor(bt[:, 3:4], bn[:, 1:2], bt[:, 1:2], ALU.subtract).then_inc(bn_v, 1)
                for g in range(GROUPS):
                    dve.wait_ge(turned, g + 1)
                    if g >= 2:
                        dve.wait_ge(mixed, g - 1)
                    nc.vector.tensor_copy(ht[g % 2][:, :], pt[g % 2][0:C, :]).then_inc(t_evac, 1)
                dve.wait_ge(gelu_done, GROUPS)
                nc.vector.tensor_reduce(mean[:, :], sums[:, :].rearrange("c (b g) -> c b g", b=B), AX_X, ALU.add).then_inc(se_mean, 1)
                dve.wait_ge(se_mean, 1)
                nc.vector.tensor_scalar(mean[:, :], mean[:, :], 1.0 / L, None, ALU.mult).then_inc(se_mean, 1)
                dve.wait_ge(se_sig, 1)
                nc.vector.tensor_scalar(gate[:, :], sig[:, :], gam[:, 0:1], None, ALU.mult)

            @block.scalar
            def _(act):
                act.wait_ge(p_in, 16 * len(loads))
                act.wait_ge(bn_s, 1)
                nc.scalar.activation(bt[:, 0:1], bn[:, 3:4], ACT.Sqrt, bias=bt[:, 4:5]).then_inc(bn_s, 1)
                act.wait_ge(bn_v, 4)
                for g in range(GROUPS):
                    b, col = g // GPB, g % GPB
                    if b >= 2 and col == 0:
                        act.wait_ge(g_out[b % 2], 16 * (b // 2))
                    act.wait_ge(mixed, g + 1)
                    nc.scalar.activation(act_out[b % 2][:, :, 8 * col:8 * col + 8].rearrange("c y x -> c x y"),
                                         pp[g % 2][0:C, :].rearrange("c (x y) -> c x y", y=H), ACT.Gelu,
                                         bias=bt[:, 3:4], scale=bt[:, 2:3], accum_out=sums[:, g:g + 1]).then_inc(gelu_done, 1)
                act.wait_ge(se_hid, 1)
                nc.scalar.activation(hid[:, :], ps[0][0:HID, 0:B], ACT.Relu, bias=b1[:, 0:1]).then_inc(se_relu, 1)
                act.wait_ge(se_out, 1)
                nc.scalar.activation(sig[:, :], ps[1][0:C, 0:B], ACT.Sigmoid, bias=b2[:, 0:1]).then_inc(se_sig, 1)


def normalise(nc, d, gate):
    NS = L // SL
    RING = 4
    with ExitStack() as ctx:
        def sb(name, shape, dt=F32):
            return ctx.enter_context(nc.sbuf_tensor(name, shape, dt))

        def sem(name):
            return ctx.enter_context(nc.semaphore(name))

        averager = sb("averager", [C, C])
        lng = sb("lng", [C, 2])
        eps = sb("ln_eps", [C, 1])
        zero = sb("zero", [C, B, HALO])
        h_in = sb("h_in", [C, RING, SL])
        x_in = sb("x_in_ln", [C, RING, SL])
        x1 = sb("x1", [C, RING, SL])
        xc = sb("xc_ln", [C, RING, SL])
        sq = sb("sq", [C, RING, SL])
        sd = sb("sd", [C, RING, SL])
        rs = sb("rs", [C, RING, SL])
        xs = sb("xs", [C, RING, SL])
        xo = sb("xo", [C, RING, SL])
        pm = [ctx.enter_context(nc.psum_tensor(f"pm{i}", [P, SL], F32)) for i in range(2)]
        pv = [ctx.enter_context(nc.psum_tensor(f"pv{i}", [P, SL], F32)) for i in range(2)]
        ln_const = sem("ln_const")
        ln_set = sem("ln_set")
        loaded = [sem(f"ln_loaded{i}") for i in range(RING)]
        stored = [sem(f"ln_stored{i}") for i in range(RING)]
        halo = sem("halo")
        added = sem("added")
        mean_ready = sem("mean_ready")
        centred = sem("centred")
        squared = sem("squared")
        var_ready = sem("var_ready")
        sd_ready = sem("sd_ready")
        rs_ready = sem("rs_ready")
        scaled = sem("scaled")
        affine = sem("affine")
        xn = d["xn_scr"]

        with nc.Block() as block:
            @block.sync
            def _(sp):
                sp.dma_start(averager[:, :], d["averager"]).then_inc(ln_const, 16)
                sp.dma_start(lng[:, 0:1], d["ln_g"].unsqueeze(1)).then_inc(ln_const, 16)
                sp.dma_start(lng[:, 1:2], d["ln_b"].unsqueeze(1)).then_inc(ln_const, 16)
                sp.wait_ge(ln_set, 1)
                sp.dma_start(xn[:, :, 0:HALO].rearrange("b c t -> c b t"), zero[:, :, :]).then_inc(halo, 16)
                sp.dma_start(xn[:, :, HALO + L:].rearrange("b c t -> c b t"), zero[:, :, :]).then_inc(halo, 16)
                with sp.Fori(0, B) as b:
                    for s in range(NS):
                        r = s % RING
                        wait(sp, added, NS * b + s - RING + 1, s >= RING - 1)
                        if s < RING - 1:
                            sp.wait_ge(added, NS * b)
                        sp.dma_start(h_in[:, r, :], d["act_scr"][b, :, s * SL:(s + 1) * SL]).then_inc(loaded[r], 16)
                        sp.dma_start(x_in[:, r, :], d["x_tok"][b, :, s * SL:(s + 1) * SL]).then_inc(loaded[r], 16)
                sp.wait_ge(halo, 32)
                for r in range(RING):
                    sp.wait_ge(stored[r], 16 * (B * NS // RING))

            @block.vector
            def _(dve):
                nc.vector.memset(eps[:, :], LN_EPS)
                nc.vector.memset(zero[:, :, :], 0.0).then_inc(ln_set, 1)

                def add(b, s):
                    r = s % RING
                    dve.wait_ge(loaded[r], 32 * (NS // RING * b + s // RING + 1))
                    wait(dve, mean_ready, NS * b + s - RING + 1, s >= RING)
                    nc.vector.scalar_tensor_tensor(x1[:, r, :], h_in[:, r, :], gate[:, bass.ds(b, 1)], x_in[:, r, :],
                                                   ALU.mult, ALU.add).then_inc(added, 1)

                def centre(b, s):
                    r = s % RING
                    dve.wait_ge(mean_ready, NS * b + s + 1)
                    dve.wait_ge(added, NS * b + s + 1)
                    wait(dve, scaled, NS * b + s - RING + 1, s >= RING)
                    nc.vector.tensor_tensor(xc[:, r, :], x1[:, r, :], pm[s % 2][0:C, :], ALU.subtract).then_inc(centred, 1)

                def invert(b, s):
                    r = s % RING
                    dve.wait_ge(sd_ready, NS * b + s + 1)
                    nc.vector.reciprocal(rs[:, r, :], sd[:, r, :]).then_inc(rs_ready, 1)

                with dve.Fori(0, B) as b:
                    dve.wait_ge(scaled, NS * b)
                    for s in range(NS + 3):
                        if s < NS:
                            add(b, s)
                        if 1 <= s <= NS:
                            centre(b, s - 1)
                        if s >= 3:
                            invert(b, s - 3)

            @block.tensor
            def _(pe):
                pe.wait_ge(ln_const, 48)
                with pe.Fori(0, B) as b:
                    pe.wait_ge(sd_ready, NS * b)
                    for s in range(NS + 2):
                        if s < NS:
                            pe.wait_ge(added, NS * b + s + 1)
                            wait(pe, centred, NS * b + s - 1, s >= 2)
                            nc.tensor.matmul(pm[s % 2][0:C, :], averager[:, :], x1[:, s % RING, :], start=True, stop=True).then_inc(mean_ready, 1)
                        if s >= 2:
                            v = s - 2
                            pe.wait_ge(squared, NS * b + v + 1)
                            wait(pe, sd_ready, NS * b + v - 1, v >= 2)
                            nc.tensor.matmul(pv[v % 2][0:C, :], averager[:, :], sq[:, v % RING, :], start=True, stop=True).then_inc(var_ready, 1)

            @block.scalar
            def _(act):
                act.wait_ge(ln_set, 1)
                act.wait_ge(ln_const, 48)
                with act.Fori(0, B) as b:
                    for s in range(NS + 4):
                        if 1 <= s <= NS:
                            v = s - 1
                            act.wait_ge(centred, NS * b + v + 1)
                            wait(act, var_ready, NS * b + v - RING + 1, v >= RING)
                            nc.scalar.activation(sq[:, v % RING, :], xc[:, v % RING, :], ACT.Square).then_inc(squared, 1)
                        if 2 <= s <= NS + 1:
                            v = s - 2
                            act.wait_ge(var_ready, NS * b + v + 1)
                            wait(act, rs_ready, NS * b + v - RING + 1, v >= RING)
                            nc.scalar.activation(sd[:, v % RING, :], pv[v % 2][0:C, :], ACT.Sqrt, bias=eps[:, 0:1]).then_inc(sd_ready, 1)
                        if s >= 4:
                            v = s - 4
                            r = v % RING
                            act.wait_ge(scaled, NS * b + v + 1)
                            act.wait_ge(stored[r], 16 * (NS // RING * b + v // RING))
                            nc.scalar.activation(xo[:, r, :], xs[:, r, :], ACT.Identity, bias=lng[:, 1:2], scale=lng[:, 0:1]).then_inc(affine, 1)
                            act.wait_ge(affine, NS * b + v + 1)
                            act.dma_start(xn[b, :, HALO + v * SL:HALO + (v + 1) * SL], xo[:, r, :]).then_inc(stored[r], 16)

            @block.gpsimd
            def _(pool):
                with pool.Fori(0, B) as b:
                    for s in range(NS):
                        r = s % RING
                        pool.wait_ge(rs_ready, NS * b + s + 1)
                        pool.wait_ge(centred, NS * b + s + 1)
                        wait(pool, affine, NS * b + s - RING + 1, s >= RING)
                        if s == 0:
                            pool.wait_ge(affine, NS * b)
                        nc.gpsimd.tensor_tensor(xs[:, r, :], xc[:, r, :], rs[:, r, :], ALU.mult).then_inc(scaled, 1)


def weights(nc, d, w):
    with ExitStack() as ctx:
        def sb(name, shape, dt=F32):
            return ctx.enter_context(nc.sbuf_tensor(name, shape, dt))

        def sem(name):
            return ctx.enter_context(nc.semaphore(name))

        w_in = sb("w_in", [HALF, DI])
        taps = sb("taps", [HALF, DCONV, DI])
        wx = sb("wx", [HALF, 2, DR + 2 * DS])
        wx_t = sb("wx_t", [DR, DI])
        wdt = sb("wdt", [DR, DI])
        spread_f = sb("spread_f", [HALF, QN * P])
        pd = [ctx.enter_context(nc.psum_tensor(f"pd{i}", [P, SL], F32)) for i in range(2)]
        w_loaded = sem("w_loaded")
        w_prod = sem("w_prod")
        a_exp = sem("a_exp")
        loads = [(w_in[:, :], d["w_in"][:, 0:DI]), (w["z"][:, :], d["w_in"][:, DI:2 * DI]),
                 (taps[:, :, :].rearrange("c k n -> c (k n)"), d["conv_taps"].partition_broadcast(HALF)),
                 (wx[:, :, :], d["w_x"]), (wx_t[:, :], d["w_x_t"]), (wdt[:, :], d["w_dt"]),
                 (spread_f[:, :], d["spread"]), (w["gather"][:, :, :].rearrange("p q n -> p (q n)"), d["gather"]),
                 (w["a"][:, :], d["a_log"]), (w["out"][:, :, :], d["w_out"]),
                 (w["conv_b"][:, :], d["conv_b"]), (w["dt_b"][:, :], d["dt_b"]), (w["skip"][:, :], d["skip"])]
        with nc.Block() as block:
            @block.sync
            def _(sp):
                for dst, src in loads:
                    sp.dma_start(dst, src).then_inc(w_loaded, 16)

            @block.scalar
            def _(act):
                act.wait_ge(w_loaded, 16 * len(loads))
                nc.scalar.activation(w["a"][:, :], w["a"][:, :], ACT.Exp).then_inc(a_exp, 1)
                act.wait_ge(a_exp, 1)
                nc.scalar.mul(w["a"][:, :], w["a"][:, :], -1.0)

            @block.tensor
            def _(pe):
                pe.wait_ge(w_loaded, 16 * len(loads))
                for h in range(2):
                    nc.tensor.matmul(pd[h][0:HALF, 0:DI], wx_t[:, h * HALF:(h + 1) * HALF], wdt[:, :], start=True, stop=True).then_inc(w_prod, 1)

            @block.vector
            def _(dve):
                dve.wait_ge(w_loaded, 16 * len(loads))
                for k in range(DCONV):
                    nc.vector.tensor_tensor(w["conv"][:, k, :], w_in[:, :], taps[:, k, :], ALU.mult)
                nc.vector.tensor_copy(w["spread"][:, :, :].rearrange("p q n -> p (q n)"), spread_f[:, :])
                for h in range(2):
                    dve.wait_ge(w_prod, h + 1)
                    nc.vector.tensor_copy(w["dt_bc"][:, h, 0:HALF], pd[h][0:HALF, 0:HALF])
                    nc.vector.tensor_copy(w["dt_bc"][:, h, HALF:P], wx[:, h, DR:])
                    nc.vector.tensor_copy(w["dt"][:, h, :], pd[h][0:HALF, HALF:DI])


def load_exp_ln(nc):
    nc.scalar.add_instruction(mybir.InstLoadActFuncSet(name=nc.get_next_instruction_name(), act_func_set_id=EXP_LN, ins=[], outs=[]))


def scan(nc, d, w):
    with ExitStack() as ctx:
        def sb(name, shape, dt=F32):
            return ctx.enter_context(nc.sbuf_tensor(name, shape, dt))

        def sem(name):
            return ctx.enter_context(nc.semaphore(name))

        def pair(name, make=None):
            return [(make or sem)(f"{name}{i}") for i in range(2)]

        NDA, NDB, NHR, NHC = 6, 2, 3, 6
        decay = [sb(f"decay{i}", [P, T]) for i in range(NDA)]
        drive = [sb(f"drive{i}", [P, T]) for i in range(NDB)]
        hring = [sb(f"hring{i}", [P, T]) for i in range(NHR)]
        hc = [sb(f"hc{i}", [P, T]) for i in range(NHC)]
        carry = sb("carry", [P, 2, UNITS])
        ends = sb("ends", [P, 3, UNITS])
        b_rep = pair("b_rep", lambda n: sb(n, [P, T]))
        c_rep = pair("c_rep", lambda n: sb(n, [P, T]))
        stack_dt = pair("stack_dt", lambda n: sb(n, [HALF, 3, T]))
        stack_u = pair("stack_u", lambda n: sb(n, [HALF, 3, T]))
        xn = sb("xn", [C, XN])
        xc = sb("xc", [HALF, 2, T])
        xa = pair("xa", lambda n: sb(n, [HALF, 2, T]))
        y_sb = sb("y_sb", [HALF, T])
        dt3 = [sb(f"dt3_{i}", [HALF, T]) for i in range(3)]
        u3 = [sb(f"u3_{i}", [HALF, T]) for i in range(3)]
        soft = sb("soft", [P, T])
        ramp = sb("ramp", [HALF, T])

        dt_ps = [ctx.enter_context(nc.psum_tensor(f"dt_ps{i}", [P, SL], F32)) for i in range(2)]
        u_ps = [ctx.enter_context(nc.psum_tensor(f"u_ps{i}", [P, SL], F32)) for i in range(3)]
        y_ps = ctx.enter_context(nc.psum_tensor("y_ps", [P, 2 * SL], F32))
        prep_ps = ctx.enter_context(nc.psum_tensor("prep_ps", [P, SL], F32))

        zeroed = sem("zeroed")
        dt_spread = sem("dt_spread")
        u_spread = sem("u_spread")
        decay_ready = sem("decay_ready")
        drive_ready = sem("drive_ready")
        scanned = sem("scanned")
        carried = sem("carried")
        c_applied = sem("c_applied")
        summed = sem("summed")
        y_ready = sem("y_ready")
        y_stored = sem("y_stored")
        xn_in = sem("xn_in")
        prep_done = sem("prep_done")
        prep_out = sem("prep_out")
        silu_done = sem("silu_done")
        soft_step = sem("soft_step")
        dt_ready = sem("dt_ready")
        u_ready = sem("u_ready")
        split = sem("split")
        bc_stored = sem("bc_stored")
        b_in = pair("b_in")
        c_in = pair("c_in")
        stack_in = pair("stack_in")

        CARRY_AT = 10
        NPREP = 8
        STACKED = 16 * 18
        SILU_AT = 2
        DT_AT = (3, 3, 4, 4, 5, 6, 7, 8)
        CONV_AT = (9, 9, 10, 11, 12, 13, 14, 14, 15, 16, 17, 18, 19, 19, 20, 21)
        CONV_OUT = tuple(CONV_AT[DCONV * g + DCONV - 1] + 1 for g in range(4))
        DT_OUT = tuple(tuple(DT_AT[4 * h + 2 * s + 1] + 1 for s in range(2)) for h in range(2))
        SUM_AT = (5, 12)
        SPLIT_AT = ((6, 7, 7, 8), (13, 14, 14, 15))

        def group(n):
            return n // HU, n % HU // 3, n % 3

        def earlier(lag, u, n, it, dr):
            if isinstance(u, int) and u < lag:
                return None
            if n >= lag:
                return u - lag, n - lag, it, dr
            return u - lag, n - lag + UNITS, it - (1 - dr), 1 - dr

        def run(eng, front, back=None, conv=None, prep=None, back_last=False, prep_first=False):
            for what, pn in ((conv, 0), (prep, 0), (conv, 1)):
                for m in range(UNITS if what else 0):
                    what(m, pn, 0, pn)
            for n in range(LEAD):
                front(n, n, 0, 0)
            with eng.Fori(0, ITERS) as it:
                for dr in range(2):
                    p = 2 * it + dr
                    nxt = (it + dr, 1 - dr)
                    for m in range(UNITS):
                        n = m + LEAD
                        where = (n, it, dr) if n < UNITS else (n - UNITS,) + nxt
                        if back and not back_last:
                            back(m, p, it, dr)
                        if prep_first:
                            for what, *part in ((prep, p + 1, *nxt), (conv, p + 2, it + 1, dr)):
                                what(m, *part)
                        front(UNITS * p + n, *where)
                        if back and back_last:
                            back(m, p, it, dr)
                        if not prep_first:
                            for what, *part in ((prep, p + 1, *nxt), (conv, p + 2, it + 1, dr)):
                                if what:
                                    what(m, *part)
                    if back:
                        back(UNITS, p, it, dr)

        with nc.Block() as block:
            @block.sync
            def _(sp):
                def load_xn(pn, img, tok):
                    wait(sp, prep_done, NPREP * (pn - 1) + 4, not isinstance(pn, int) or pn > 0)
                    sp.dma_start(xn[:, :], d["xn_scr"][img, :, bass.ds(tok, XN)]).then_inc(xn_in, 16)

                def prep_loads(pn, it, dr):
                    sp.wait_ge(prep_out, NPREP * pn + 6)
                    sp.dma_start(d["bc_scr"][dr], soft[HALF:P, :]).then_inc(bc_stored, 16)
                    first = isinstance(pn, int)
                    if not first:
                        sp.wait_ge(c_applied, UNITS * (pn - 1))
                    sp.wait_ge(bc_stored, 16 * (pn + 1))
                    for dst, lo, s in ((b_rep, 0, b_in), (c_rep, DS, c_in)):
                        sp.dma_start(dst[dr][:, :], d["bc_scr"][dr][lo:lo + DS, :].partition_broadcast(GC)).then_inc(s[dr], 16)
                    for h in range(2):
                        for parts, i, dst, made, per, step in ((dt3, 0, stack_dt, dt_ready, 1, 1), (u3, 0, stack_u, u_ready, 1, 1),
                                                               (dt3, 1, stack_dt, split, 4, 1), (dt3, 2, stack_dt, split, 4, 2),
                                                               (u3, 1, stack_u, split, 4, 3), (u3, 2, stack_u, split, 4, 4)):
                            sp.wait_ge(made, 2 * per * pn + (per * h + step))
                            if not first and made is dt_ready:
                                sp.wait_ge(u_spread, 2 * (UNITS * (pn - 1) + HU * (h + 1)))
                            for j in range(3):
                                sp.dma_start(dst[h][32 * i:32 * i + 32, j, :], parts[i][32 * j:32 * j + 32, :]).then_inc(stack_in[h], 16)
                        yield h

                def tokens(it, dr):
                    return it % CHUNKS * T if dr == 0 else it % CHUNKS * -T + (CHUNKS - 1) * T

                load_xn(0, 0, tokens(0, 0))
                load_xn(1, 0, tokens(0, 1))
                for _ in prep_loads(0, 0, 0):
                    pass
                load_xn(2, 0, tokens(1, 0))
                with sp.Fori(0, ITERS) as it:
                    for dr in range(2):
                        p = 2 * it + dr
                        after = (it + (1 + dr)) % ITERS
                        img, img3 = it // CHUNKS, after // CHUNKS
                        tok, tok3 = tokens(it, dr), tokens(after, 1 - dr)
                        for h in prep_loads(p + 1, it + dr, 1 - dr):
                            if h == 1:
                                load_xn(p + 3, img3, tok3)
                            sp.wait_ge(y_ready, 2 * p + h + 1)
                            sp.dma_start(d["y_scr"][dr][img, h * HALF:(h + 1) * HALF, bass.ds(tok, T)],
                                         y_sb[:, :]).then_inc(y_stored, 16)
                sp.wait_ge(y_stored, 16 * 4 * ITERS)
                sp.wait_ge(xn_in, 16 * (2 * ITERS + 3))
                for h in range(2):
                    sp.wait_ge(stack_in[h], STACKED * (2 * ITERS + 1))
                sp.wait_ge(b_in[0], 16 * (ITERS + 1))
                sp.wait_ge(c_in[0], 16 * (ITERS + 1))

            @block.tensor
            def _(pe):
                def spread(dst, stack, n, i):
                    h, q, j = group(n)
                    return nc.tensor.matmul(dst[:, :], w["spread"][:, q, :], upper(stack[h][:, j, i * SL:(i + 1) * SL]),
                                            start=True, stop=True)

                def front(u, n, it, dr):
                    if (was := earlier(2, u, n, it, dr)) is not None:
                        v, nv, _, _ = was
                        for i in range(2):
                            wait(pe, drive_ready, 2 * v + i - 2, not isinstance(v, int) or 2 * v + i - 2 > 0)
                            spread(u_ps[(2 * nv + i) % 3], stack_u, nv, i).then_inc(u_spread, 1)
                    if n % HU == 0:
                        pe.wait_ge(stack_in[n // HU], STACKED * (2 * it + dr + 1))
                    for i in range(2):
                        wait(pe, decay_ready, 2 * (u - 1) + i + 1, u)
                        spread(dt_ps[i], stack_dt, n, i).then_inc(dt_spread, 1)

                def back(m, p, it, dr):
                    i = m % 3 - 1
                    if m == UNITS or i < 0:
                        return
                    n0 = m // 3 * 3
                    if i == 0:
                        pe.wait_ge(c_applied, UNITS * p + n0 + 3)
                        if n0 % HU == 0:
                            pe.wait_ge(y_ready, 2 * p + n0 // HU)
                    for n in range(n0, n0 + 3):
                        h, q, j = group(n)
                        last = nc.tensor.matmul(y_ps[32 * j:32 * j + 32, i * SL:(i + 1) * SL], w["gather"][:, q, :],
                                                hc[n % NHC][:, i * SL:(i + 1) * SL], start=(q == 0), stop=(q == QN - 1))
                    if i == 1:
                        last.then_inc(summed, 3)

                def product(k, pn, it, dr):
                    if k < 4 * DCONV:
                        g, tap = divmod(k, DCONV)
                        h, s = divmod(g, 2)
                        if k == 0:
                            pe.wait_ge(xn_in, 16 * (pn + 1))
                        if tap == 0:
                            wait(pe, prep_out, NPREP * pn + g, not isinstance(pn, int) or pn + g > 0)
                        at = s * SL + (tap if dr == 0 else 2 * HALO - tap)
                        mm = nc.tensor.matmul(prep_ps[0:HALF, :], w["conv"][:, tap, h * HALF:(h + 1) * HALF],
                                              xn[:, at:at + SL], start=(tap == 0), stop=(tap == DCONV - 1))
                        if tap == DCONV - 1:
                            mm.then_inc(prep_done, 1)
                        return
                    g, part = divmod(k - 4 * DCONV, 2)
                    h, s = divmod(g, 2)
                    if part == 0:
                        pe.wait_ge(silu_done, pn + 1)
                        pe.wait_ge(prep_out, NPREP * pn + 4 + g)
                    mat, rows = (w["dt"], HALF) if h else (w["dt_bc"], P)
                    mm = nc.tensor.matmul(prep_ps[0:rows, :], mat[:, part, :], xa[dr][:, part, s * SL:(s + 1) * SL],
                                          start=(part == 0), stop=(part == 1))
                    if part == 1:
                        mm.then_inc(prep_done, 1)

                def conv(m, pn, it, dr):
                    for k, at in enumerate(CONV_AT):
                        if at == m:
                            product(k, pn, it, dr)

                def prep(m, pn, it, dr):
                    for k, at in enumerate(DT_AT):
                        if at == m:
                            product(4 * DCONV + k, pn, it, dr)

                run(pe, front, back, conv, prep, back_last=True)

            @block.scalar
            def _(act):
                def front(u, n, it, dr):
                    h, q, j = group(n)
                    col = h * HU + j * QN + q
                    wait(act, scanned, u - NDA + 1, not isinstance(u, int) or u >= NDA)
                    if n == CARRY_AT:
                        was = earlier(CARRY_AT + 1, u, n, it, dr)
                        act.wait_ge(c_applied, u - CARRY_AT)
                    for i in range(2):
                        act.wait_ge(dt_spread, 2 * u + i + 1)
                        nc.scalar.activation(decay[n % NDA][:, i * SL:(i + 1) * SL], dt_ps[i][:, :], ACT.Exp,
                                             scale=w["a"][:, col:col + 1]).then_inc(decay_ready, 1)
                    if n == CARRY_AT:
                        _, _, itv, drv = was
                        at = drv * UNITS + (itv % CHUNKS) // (CHUNKS - 1) * ((2 - drv) * UNITS)
                        nc.scalar.copy(carry[:, drv, :], ends[:, :, :].rearrange("p d n -> p (d n)")[:, bass.ds(at, UNITS)]).then_inc(carried, 1)

                def conv(m, pn, it, dr):
                    if m in CONV_OUT:
                        g = CONV_OUT.index(m)
                        h, s = divmod(g, 2)
                        wait(act, silu_done, pn, pn)
                        act.wait_ge(prep_done, NPREP * pn + g + 1)
                        nc.scalar.activation(xc[:, h, s * SL:(s + 1) * SL], prep_ps[0:HALF, :], ACT.Identity,
                                             bias=w["conv_b"][:, h:h + 1]).then_inc(prep_out, 1)

                def prep(m, pn, it, dr):
                    if m == SILU_AT:
                        wait(act, y_ready, 2 * (pn - 1), pn)
                        act.wait_ge(prep_out, NPREP * pn + 4)
                        nc.scalar.activation(xa[dr][:, :, :], xc[:, :, :], ACT.Silu).then_inc(silu_done, 1)
                        load_exp_ln(nc)
                    for h in range(2):
                        if m in DT_OUT[h]:
                            s = DT_OUT[h].index(m)
                            act.wait_ge(prep_done, NPREP * pn + 4 + 2 * h + s + 1)
                            if s == 0:
                                wait(act, dt_ready, 2 * pn + h, not isinstance(pn, int) or h > 0)
                            sl = slice(s * SL, (s + 1) * SL)
                            if h == 0:
                                if s == 0:
                                    wait(act, bc_stored, 16 * pn, pn)
                                nc.scalar.copy(soft[HALF:P, sl], prep_ps[HALF:P, :])
                            nc.scalar.activation(soft[0:HALF, sl], prep_ps[0:HALF, :], ACT.Abs, bias=w["dt_b"][:, h:h + 1])
                            nc.scalar.activation(ramp[:, sl], prep_ps[0:HALF, :], ACT.Relu, bias=w["dt_b"][:, h:h + 1]).then_inc(prep_out, 1)
                            if s == 1:
                                act.wait_ge(prep_out, NPREP * pn + 4 + 2 * h + 2)
                                nc.scalar.activation(soft[0:HALF, :], soft[0:HALF, :], ACT.Exp, scale=-1.0).then_inc(soft_step, 1)
                                act.wait_ge(soft_step, 2 * (2 * pn + h) + 1)
                                nc.scalar.activation(soft[0:HALF, :], soft[0:HALF, :], ACT.Ln, bias=1.0).then_inc(soft_step, 1)

                act.wait_ge(zeroed, 1)
                load_exp_ln(nc)
                run(act, front, None, conv, prep, prep_first=True)

            @block.vector
            def _(dve):
                nc.vector.memset(ends[:, 0:2, :], 0.0)
                nc.vector.memset(carry[:, :, :], 0.0).then_inc(summed, NHC)
                nc.vector.memset(ends[:, 2, :], 0.0).then_inc(zeroed, 1)
                dve.wait_ge(zeroed, 1)

                def front(u, n, it, dr):
                    if (was := earlier(2, u, n, it, dr)) is None:
                        return
                    v, nv, itv, drv = was
                    if nv == 0:
                        dve.wait_ge(b_in[drv], 16 * (itv + 1))
                    wait(dve, scanned, v - NDB + 1, not isinstance(v, int) or v >= NDB)
                    for i in range(2):
                        dve.wait_ge(u_spread, 2 * v + i + 1)
                        sl = slice(i * SL, (i + 1) * SL)
                        nc.vector.tensor_tensor(drive[nv % NDB][:, sl], u_ps[(2 * nv + i) % 3][:, :], b_rep[drv][:, sl],
                                                ALU.mult).then_inc(drive_ready, 1)
                    if (was := earlier(3, u, n, it, dr)) is None:
                        return
                    v, nv, itv, drv = was
                    dve.wait_ge(decay_ready, 2 * v + 2)
                    dve.wait_ge(drive_ready, 2 * v + 2)
                    wait(dve, c_applied, v - NHR + 1, not isinstance(v, int) or v >= NHR)
                    if nv == 0:
                        wait(dve, carried, 2 * itv + drv - 1, not isinstance(v, int))
                    r = nv % NHR
                    step = 1 if drv == 0 else -1
                    nc.vector.tensor_tensor_scan(hring[r][:, ::step], decay[nv % NDA][:, ::step],
                                                 drive[nv % NDB][:, ::step], carry[:, drv, nv:nv + 1],
                                                 ALU.mult, ALU.add).then_inc(scanned, 1)

                def back(n, p, it, dr):
                    if n == 0 or n % HU:
                        return
                    h = n // HU - 1
                    dve.wait_ge(summed, NHC + UNITS * p + n)
                    dve.wait_ge(y_stored, 16 * (2 * p + h))
                    nc.vector.scalar_tensor_tensor(y_sb[:, :], xa[dr][:, h, :], w["skip"][:, h:h + 1], y_ps[0:HALF, :],
                                                   ALU.mult, ALU.add).then_inc(y_ready, 1)

                def prep(m, pn, it, dr):
                    for h in range(2):
                        for i, (parts, ready) in enumerate(((dt3, dt_ready), (u3, u_ready))):
                            for k in range(2):
                                if m == SPLIT_AT[h][2 * i + k]:
                                    count = 4 * (2 * pn + h) + 2 * i + k
                                    dve.wait_ge(ready, 2 * pn + h + 1)
                                    if k == 1:
                                        dve.wait_ge(split, count)
                                    nc.vector.tensor_tensor(parts[k + 1][:, :], parts[k][:, :], upper(parts[k][:, :]),
                                                            ALU.subtract).then_inc(split, 1)

                run(dve, front, back, None, prep)

            @block.gpsimd
            def _(pool):
                def front(u, n, it, dr):
                    if (was := earlier(3, u, n, it, dr)) is None:
                        return
                    v, nv, itv, drv = was
                    if nv == 0:
                        pool.wait_ge(c_in[drv], 16 * (itv + 1))
                        wait(pool, carried, 2 * itv + drv - 1, not isinstance(v, int))
                    pool.wait_ge(scanned, v + 1)
                    pool.wait_ge(summed, v + 1)
                    r = nv % NHR
                    end = T - 1 if drv == 0 else 0
                    nc.gpsimd.tensor_tensor(hc[nv % NHC][:, :], hring[r][:, :], c_rep[drv][:, :], ALU.mult)
                    nc.gpsimd.tensor_copy(ends[:, drv, nv:nv + 1], hring[r][:, end:end + 1]).then_inc(c_applied, 1)

                def prep(m, pn, it, dr):
                    for h in range(2):
                        if m == SUM_AT[h]:
                            pool.wait_ge(soft_step, 2 * (2 * pn + h) + 2)
                            wait(pool, stack_in[1 - h], STACKED * (pn + h), not isinstance(pn, int) or h > 0)
                            nc.gpsimd.tensor_tensor(dt3[0][:, :], soft[0:HALF, :], ramp[:, :], ALU.add).then_inc(dt_ready, 1)
                        if m == SUM_AT[h] + 1:
                            pool.wait_ge(dt_ready, 2 * pn + h + 1)
                            pool.wait_ge(silu_done, pn + 1)
                            nc.gpsimd.tensor_tensor(u3[0][:, :], dt3[0][:, :], xa[dr][:, h, :], ALU.mult).then_inc(u_ready, 1)

                run(pool, front, None, None, prep)


def output(nc, d, w):
    NS = L // SL
    with ExitStack() as ctx:
        def sb(name, shape, dt=F32):
            return ctx.enter_context(nc.sbuf_tensor(name, shape, dt))

        def sem(name):
            return ctx.enter_context(nc.semaphore(name))

        R = 4
        yf = sb("yf", [HALF, R, 2, SL])
        yb = sb("yb", [HALF, R, 2, SL])
        xz = sb("xz", [C, R, SL])
        ys = sb("ys", [HALF, R, 2, SL])
        sz = sb("sz", [HALF, R, 2, SL])
        yg = sb("yg", [HALF, R, 2, SL])
        res = sb("res", [C, R, SL])
        pz = [ctx.enter_context(nc.psum_tensor(f"pz{i}", [P, 2 * SL], F32)) for i in range(2)]
        po = [ctx.enter_context(nc.psum_tensor(f"po{i}", [P, SL], F32)) for i in range(2)]
        o_loaded = [sem(f"o_loaded{i}") for i in range(R)]
        o_stored = [sem(f"o_stored{i}") for i in range(R)]
        y_sum = sem("y_sum")
        z_made = sem("z_made")
        z_silu = sem("z_silu")
        gated = sem("gated")
        projected = sem("projected")
        res_ready = sem("res_ready")
        with nc.Block() as block:
            @block.sync
            def _(sp):
                with sp.Fori(0, B) as b:
                    for s in range(NS):
                        r = s % R
                        if s >= R:
                            sp.wait_ge(y_sum, NS * b + s - R + 1)
                            sp.wait_ge(z_made, NS * b + s - R + 1)
                        elif s == 0:
                            sp.wait_ge(y_sum, NS * b)
                            sp.wait_ge(z_made, NS * b)
                        sl = slice(s * SL, (s + 1) * SL)
                        for t, src in ((yf, d["y_scr"][0]), (yb, d["y_scr"][1])):
                            sp.dma_start(t[:, r, :, :], src[b, :, sl].rearrange("(h c) t -> c h t", h=2)).then_inc(o_loaded[r], 16)
                        sp.dma_start(xz[:, r, :], d["xn_scr"][b, :, HALO + s * SL:HALO + (s + 1) * SL]).then_inc(o_loaded[r], 16)
                for r in range(R):
                    sp.wait_ge(o_stored[r], 16 * (B * NS // R))

            @block.gpsimd
            def _(pool):
                with pool.Fori(0, B) as b:
                    for s in range(NS):
                        r = s % R
                        pool.wait_ge(o_loaded[r], 48 * (NS // R * b + s // R + 1))
                        if s >= R:
                            pool.wait_ge(gated, NS * b + s - R + 1)
                        elif s == 0:
                            pool.wait_ge(gated, NS * b)
                        nc.gpsimd.tensor_tensor(ys[:, r, :, :], yf[:, r, :, :], yb[:, r, :, :], ALU.add).then_inc(y_sum, 1)

            @block.tensor
            def _(pe):
                with pe.Fori(0, B) as b:
                    pe.wait_ge(z_silu, NS * b)
                    pe.wait_ge(res_ready, NS * b)
                    for s in range(NS + 1):
                        if s < NS:
                            pe.wait_ge(o_loaded[s % R], 48 * (NS // R * b + s // R + 1))
                            wait(pe, z_silu, NS * b + s - 1, s >= 2)
                            for h in range(2):
                                last = nc.tensor.matmul(pz[s % 2][0:HALF, h * SL:(h + 1) * SL], w["z"][:, h * HALF:(h + 1) * HALF],
                                                        xz[:, s % R, :], start=True, stop=True)
                            last.then_inc(z_made, 1)
                        if s >= 1:
                            v = s - 1
                            pe.wait_ge(gated, NS * b + v + 1)
                            wait(pe, res_ready, NS * b + v - 1, v >= 2)
                            for h in range(2):
                                last = nc.tensor.matmul(po[v % 2][0:C, :], w["out"][:, h, :], yg[:, v % R, h, :], start=(h == 0), stop=(h == 1))
                            last.then_inc(projected, 1)

            @block.scalar
            def _(act):
                with act.Fori(0, B) as b:
                    act.wait_ge(gated, NS * b)
                    for s in range(NS + 2):
                        if s < NS:
                            act.wait_ge(z_made, NS * b + s + 1)
                            wait(act, gated, NS * b + s - R + 1, s >= R)
                            nc.scalar.activation(sz[:, s % R, :, :].rearrange("p h t -> p (h t)"), pz[s % 2][0:HALF, :], ACT.Silu).then_inc(z_silu, 1)
                        if s >= 2:
                            v = s - 2
                            r = v % R
                            act.wait_ge(projected, NS * b + v + 1)
                            act.wait_ge(o_stored[r], 16 * (NS // R * b + v // R))
                            nc.scalar.copy(res[:, r, :], po[v % 2][0:C, :]).then_inc(res_ready, 1)
                            act.wait_ge(res_ready, NS * b + v + 1)
                            act.dma_start(d["out"][b, :, v * SL:(v + 1) * SL], res[:, r, :]).then_inc(o_stored[r], 16)

            @block.vector
            def _(dve):
                with dve.Fori(0, B) as b:
                    dve.wait_ge(projected, NS * b)
                    for s in range(NS):
                        r = s % R
                        dve.wait_ge(y_sum, NS * b + s + 1)
                        dve.wait_ge(z_silu, NS * b + s + 1)
                        wait(dve, projected, NS * b + s - R + 1, s >= R)
                        nc.vector.tensor_tensor(yg[:, r, :, :], ys[:, r, :, :], sz[:, r, :, :], ALU.mult).then_inc(gated, 1)


def mixer_weights(nc, ctx):
    shapes = {"conv": ([HALF, DCONV, DI], F32), "dt_bc": ([HALF, 2, P], F32), "dt": ([HALF, 2, HALF], F32),
              "z": ([C, DI], F32), "out": ([HALF, 2, C], F32), "a": ([P, UNITS], F32),
              "spread": ([HALF, QN, P], BF16), "gather": ([P, QN, 32], F32),
              "conv_b": ([HALF, 2], F32), "dt_b": ([HALF, 2], F32), "skip": ([HALF, 2], F32)}
    return {n: ctx.enter_context(nc.sbuf_tensor("w_" + n, s, t)) for n, (s, t) in shapes.items()}


def vision_mixer_kernel(nc, d):
    d["act_scr"] = nc.dram_tensor("act_scr", [B, C, L], F32, kind="Internal").ap()
    d["xn_scr"] = nc.dram_tensor("xn_scr", [B, C, L + 2 * HALO], F32, kind="Internal").ap()
    d["y_scr"] = [nc.dram_tensor(f"y_scr{i}", [B, DI, L], F32, kind="Internal").ap() for i in range(2)]
    d["bc_scr"] = [nc.dram_tensor(f"bc_scr{i}", [2 * DS, T], F32, kind="Internal").ap() for i in range(2)]
    with nc.sbuf_tensor("gate", [C, B], F32) as gate:
        with nc.sbuf_tensor("hs", [P, C * B * XH], F32) as hs:
            convolution(nc, d, hs)
            pointwise(nc, d, hs, gate)
        normalise(nc, d, gate)
    with ExitStack() as ctx:
        w = mixer_weights(nc, ctx)
        weights(nc, d, w)
        scan(nc, d, w)
        output(nc, d, w)


def layout(inputs):
    import numpy as np
    f = {k: np.ascontiguousarray(v) for k, v in inputs.items()}
    x = f["x"]
    d = {}
    d["x_cols"] = x.reshape(B, C, H, XH, 2).transpose(4, 2, 1, 0, 3).reshape(P, C, B, XH)
    d["x_tok"] = x.reshape(B, C, L)
    fp = np.pad(f["L0_conv_plk_filter"].reshape(C, K, K), ((0, 0), (0, 0), (1, 1)))
    cols = np.empty((2, K, C, SHIFTS, 2), np.float32)
    for pi in range(2):
        for po in range(2):
            for s in range(SHIFTS):
                cols[pi, :, :, s, po] = fp[:, :, 2 * s + pi - po + 1].T
    d["filter_cols"] = cols.reshape(FROWS, C * FCOLS)
    band = np.zeros((3, 2, K, 2, 2 * H - 1), np.float32)
    for pi in range(2):
        for dy in range(K):
            band[:, pi, dy, pi, H - 1 + dy - PAD] = 1.0
    d["band"] = band.reshape(3 * FROWS, -1)
    m = np.zeros((3, FROWS, 2), np.float32)
    m[1:, :, 0] = -1.0
    m[2:, :, 1] = -1.0
    d["split_masks"] = m.reshape(3 * FROWS, 2)
    for n in ("gamma", "beta", "mean", "var"):
        d["bn1_" + n] = f["L0_conv_bn1_" + n]
        d["bn2_" + n] = f["L0_conv_bn2_" + n]
    d["ident"] = np.eye(P, dtype=np.float32)
    d["pw_t"] = f["L0_conv_pw_weight"].T
    d["se_w1_t"] = f["L0_conv_se_w1"].T
    d["se_w2_t"] = f["L0_conv_se_w2"].T
    d["se_b1"] = f["L0_conv_se_b1"]
    d["se_b2"] = f["L0_conv_se_b2"]
    d["gamma"] = f["L0_conv_gamma"]
    d["averager"] = np.full((C, C), 1.0 / C, np.float32)
    d["ln_g"] = f["L1_conv_ln_g"]
    d["ln_b"] = f["L1_conv_ln_b"]
    d["w_in"] = f["L1_conv_W_in"]
    d["conv_taps"] = f["L1_conv_conv_w"].T.reshape(-1)
    d["w_x"] = f["L1_conv_W_xproj"].reshape(2, HALF, -1).transpose(1, 0, 2)
    d["w_x_t"] = f["L1_conv_W_xproj"][:, :DR].T
    d["w_dt"] = f["L1_conv_W_dt"]
    d["a_log"] = f["L1_conv_A_log"].reshape(UNITS, P).T
    d["w_out"] = f["L1_conv_W_out"].reshape(2, HALF, C).transpose(1, 0, 2)
    d["conv_b"] = f["L1_conv_conv_b"].reshape(2, HALF).T
    d["dt_b"] = f["L1_conv_b_dt"].reshape(2, HALF).T
    d["skip"] = f["L1_conv_D"].reshape(2, HALF).T
    spread = np.zeros((3, 32, QN, GC, DS), np.float32)
    gather = np.zeros((GC, DS, QN, 32), np.float32)
    for r in range(32):
        spread[:, r, r // GC, r % GC, :] = 1.0
        gather[r % GC, :, r // GC, r] = 1.0
    d["spread"] = spread.reshape(HALF, QN * P)
    d["gather"] = gather.reshape(P, QN * 32)
    return {k: np.ascontiguousarray(v) for k, v in d.items()}


def kernel(**inputs):
    import numpy as np
    import concourse.bacc as bacc
    from concourse.bass_utils import run_bass_kernel_spmd

    nc = bacc.Bacc("TRN2", target_bir_lowering=False, num_devices=1)
    arrays, drams = {}, {}
    for name, a in layout({k: np.asarray(v) for k, v in inputs.items()}).items():
        arrays["in_" + name] = a
        drams[name] = nc.dram_tensor("in_" + name, a.shape, mybir.dt.from_np(a.dtype), kind="ExternalInput").ap()
    drams["out"] = nc.dram_tensor("out", (B, C, L), F32, kind="ExternalOutput").ap()
    vision_mixer_kernel(nc, drams)
    result = run_bass_kernel_spmd(nc, [arrays], core_ids=[0])
    return result.results[0]["out"].reshape(B, C, H, W)
```

```python
from contextlib import ExitStack
from functools import partial

import concourse.bass as bass
from concourse import mybir

F32 = mybir.dt.float32
BF16 = mybir.dt.bfloat16
ALU = mybir.AluOpType
ACT = mybir.ActivationFunctionType
AX_X = mybir.AxisListType.X

P = 128
B, C, H, W = 8, 96, 64, 64
L = H * W
BN_EPS = 1e-5
LN_EPS = 1e-5

K = 17
PAD = K // 2
XH = W // 2
SHIFTS = PAD + 1
NEAR = PAD // 2
XP = XH + 2 * NEAR
CB = 4
BATCHES = C // CB
FCOLS = SHIFTS * 2
FROWS = 2 * K
YG = 4
NYG = H // YG

DI = 192
HALF = DI // 2
DS = 16
DR = 6
DCONV = 4
T = 1024
SL = 512
NS = L // SL
CHUNKS = L // T
HALO = DCONV - 1
XN = T + 2 * HALO
GC = P // DS
UNITS = DI // GC
HU = UNITS // 2
QN = 32 // GC
ITERS = B * CHUNKS
EXP_LN = 6
LEAD = 6


def upper(ap):
    return ap.bitcast(BF16)[:, 1::2]



def wait(eng, sem, count, when=True):
    if when is True or not isinstance(when, (bool, int)) or when:
        eng.wait_ge(sem, count)


def over_slices(eng, *stages):
    most = max(lead for lead, _ in stages)

    def image(b, last=False):
        for s in range(NS):
            for lead, what in stages:
                if s + lead < NS:
                    what(b, s + lead)
                elif not last:
                    what(b + 1, s + lead - NS)

    for s in range(most):
        for lead, what in stages:
            if s >= most - lead:
                what(0, s - (most - lead))
    image(0)
    with eng.Fori(1, B - 1) as b:
        image(b)
    image(B - 1, last=True)


def after(eng, sem, count):
    if not isinstance(count, int) or count > 0:
        eng.wait_ge(sem, count)


def load_exp_ln(nc):
    nc.scalar.add_instruction(mybir.InstLoadActFuncSet(name=nc.get_next_instruction_name(), act_func_set_id=EXP_LN, ins=[], outs=[]))


def convolution(nc, d, hs):
    with ExitStack() as ctx:
        def sb(name, shape, dt=F32):
            return ctx.enter_context(nc.sbuf_tensor(name, shape, dt))

        def sem(name):
            return ctx.enter_context(nc.semaphore(name))

        filt = sb("filt", [3 * FROWS, (C + CB) * FCOLS])
        filt_tmp = hs[0:3 * FROWS, 0:C * FCOLS]
        masks = sb("masks", [3 * FROWS, 2])
        band_f = sb("band_f", [3 * FROWS, 2 * (2 * H - 1)])
        band = sb("band", [3 * FROWS, 2, 2 * H - 1], BF16)
        bands = sb("bands", [3 * FROWS, H, P], BF16)
        toep = [sb(f"toep{i}", [P, CB * FCOLS, H]) for i in range(2)]
        xraw = [sb(f"xraw{i}", [P, CB, B, XH]) for i in range(2)]
        xpad = [sb(f"xpad{i}", [P, CB, B, XP]) for i in range(2)]
        bnp = sb("bnp", [P, 4, C])
        bnt = sb("bnt", [P, 3, C])
        scale = sb("scale", [P, C])
        shift = sb("shift", [P, C])
        eps = sb("eps", [P, 1])
        pw = [ctx.enter_context(nc.psum_tensor(f"pw{i}", [P, SL], F32)) for i in range(2)]
        pc = [ctx.enter_context(nc.psum_tensor(f"pc{i}", [P, SL], F32)) for i in range(CB)]

        const_in = sem("const_in")
        x_in = [sem(f"x_in{i}") for i in range(2)]
        eps_set = sem("eps_set")
        bn_sqrt = sem("bn_sqrt")
        bn_dve = sem("bn_dve")
        filt_step = sem("filt_step")
        band_ready = sem("band_ready")
        pads_zero = sem("pads_zero")
        x_ready = sem("x_ready")
        w_ready = sem("w_ready")
        w_evac = [sem(f"w_evac{i}") for i in range(2)]
        conv_done = [sem(f"conv_done{i}") for i in range(2)]
        h_evac = [sem(f"h_evac{i}") for i in range(CB)]

        xk = d["x_cols"]
        NCONST = 3 + 3 + 4
        after = [range(NYG // CB * i, NYG // CB * (i + 1)) for i in range(CB)]

        with nc.Block() as block:
            @block.sync
            def _(sp):
                for i in range(3):
                    sp.dma_start(filt[i * FROWS:(i + 1) * FROWS, 0:C * FCOLS], d["filter_cols"]).then_inc(const_in, 16)
                sp.dma_start(band_f[:, :], d["band"]).then_inc(const_in, 16)
                sp.dma_start(masks[:, :], d["split_masks"]).then_inc(const_in, 16)
                for i, name in enumerate(("gamma", "beta", "mean", "var")):
                    sp.dma_start(bnp[:, i, :], d["bn1_" + name].partition_broadcast(P)).then_inc(const_in, 16)
                for i in range(2):
                    sp.dma_start(xraw[i][:, :, :, :], xk[:, i * CB:(i + 1) * CB, :, :]).then_inc(x_in[i], 16)
                with sp.Fori(0, BATCHES // 2) as i:
                    for par in range(2):
                        ch = (2 * i + par + 2) % BATCHES * CB
                        sp.wait_ge(x_ready, 2 * i + par + 1)
                        sp.dma_start(xraw[par][:, :, :, :], xk[:, bass.ds(ch, CB), :, :]).then_inc(x_in[par], 16)
                for i in range(2):
                    sp.wait_ge(x_in[i], 16 * (BATCHES // 2 + 1))

            def place_bands(eng, rows):
                for y in rows:
                    last = eng.tensor_copy(bands[:, y, :].rearrange("p (a b) -> p a b", a=2), band[:, :, H - 1 - y:2 * H - 1 - y])
                last.then_inc(band_ready, 1)

            @block.gpsimd
            def _(pool):
                for i in range(2):
                    nc.gpsimd.memset(xpad[i][:, :, :, 0:NEAR], 0.0)
                    last = nc.gpsimd.memset(xpad[i][:, :, :, NEAR + XH:XP], 0.0)
                last.then_inc(pads_zero, 1)
                pool.wait_ge(band_ready, 1)
                place_bands(nc.gpsimd, range(3 * H // 4, H))

            def evacuate_weights(eng, copy, s, buf, bank, yg, batches_before):
                if batches_before is not None:
                    eng.wait_ge(conv_done[buf], CB * batches_before)
                eng.wait_ge(w_ready, NYG * s + yg + 1)
                src = pw[bank][:, 0:YG * CB * FCOLS].rearrange("p (y n) -> p n y", y=YG)
                copy(toep[buf][:, :, yg * YG:(yg + 1) * YG], src).then_inc(w_evac[bank], 1)

            def evacuate_conv(eng, copy, i, par, c):
                s = 2 * i + par
                eng.wait_ge(conv_done[par], CB * i + c + 1)
                copy(hs[:, bass.ds((CB * s + c) * B * XH, B * XH)], pc[c][:, 0:B * XH]).then_inc(h_evac[c], 1)

            def evacuations(eng, copy, mine, norm=None):
                for yg in range(mine, NYG, 2):
                    evacuate_weights(eng, copy, 0, 0, mine, yg, None)
                with eng.Fori(0, BATCHES // 2) as i:
                    for par in range(2):
                        s = 2 * i + par
                        for c in range(CB):
                            for yg in after[c]:
                                if yg % 2 == mine:
                                    evacuate_weights(eng, copy, s + 1, 1 - par, mine, yg, i + par)
                            if c % 2 == mine:
                                evacuate_conv(eng, copy, i, par, c)
                            if norm and c == 1:
                                norm(i, par)

            @block.scalar
            def _(act):
                act.wait_ge(const_in, 16 * (NCONST - 1))
                act.wait_ge(eps_set, 1)
                nc.scalar.activation(bnt[:, 0, :], bnp[:, 3, :], ACT.Sqrt, bias=eps[:, 0:1]).then_inc(bn_sqrt, 1)
                evacuations(act, nc.scalar.copy, 0)

            @block.vector
            def _(dve):
                nc.vector.memset(filt[:, C * FCOLS:], 0.0)
                nc.vector.memset(eps[:, :], BN_EPS).then_inc(eps_set, 1)
                dve.wait_ge(const_in, 16 * (NCONST - 1))
                nc.vector.tensor_copy(band[:, :, :].rearrange("p a b -> p (a b)"), band_f[:, :]).then_inc(band_ready, 1)
                dve.wait_ge(band_ready, 1)
                place_bands(nc.vector, range(0, 3 * H // 4))
                f = filt[:, 0:C * FCOLS]
                nc.vector.scalar_tensor_tensor(filt_tmp, upper(f), masks[:, 0:1], f, ALU.mult, ALU.add).then_inc(filt_step, 1)
                dve.wait_ge(filt_step, 1)
                nc.vector.scalar_tensor_tensor(f, upper(filt_tmp), masks[:, 1:2], filt_tmp, ALU.mult, ALU.add).then_inc(filt_step, 1)
                dve.wait_ge(bn_sqrt, 1)
                nc.vector.reciprocal(bnt[:, 1, :], bnt[:, 0, :]).then_inc(bn_dve, 1)
                dve.wait_ge(bn_dve, 1)
                nc.vector.tensor_tensor(scale[:, :], bnt[:, 1, :], bnp[:, 0, :], ALU.mult).then_inc(bn_dve, 1)
                dve.wait_ge(bn_dve, 2)
                nc.vector.tensor_tensor(bnt[:, 2, :], scale[:, :], bnp[:, 2, :], ALU.mult).then_inc(bn_dve, 1)
                dve.wait_ge(bn_dve, 3)
                nc.vector.tensor_tensor(shift[:, :], bnp[:, 1, :], bnt[:, 2, :], ALU.subtract).then_inc(bn_dve, 2)
                dve.wait_ge(filt_step, 2)
                dve.wait_ge(bn_dve, 5)
                dve.wait_ge(pads_zero, 1)

                def batch_norm(s, buf, loads):
                    dve.wait_ge(x_in[buf], 16 * loads)
                    for c in range(CB):
                        at = s * CB + c
                        last = nc.vector.tensor_scalar(xpad[buf][:, c, :, NEAR:NEAR + XH], xraw[buf][:, c, :, :],
                                                       scale[:, bass.ds(at, 1)], shift[:, bass.ds(at, 1)], ALU.mult, ALU.add)
                    last.then_inc(x_ready, 1)

                def next_norm(i, par):
                    wait(dve, conv_done[1 - par], CB * (i + par), True)
                    batch_norm((2 * i + par + 1) % BATCHES, 1 - par, i + par + 1)

                batch_norm(0, 0, 1)
                evacuations(dve, nc.vector.tensor_copy, 1, next_norm)

            @block.tensor
            def _(pe):
                pe.wait_ge(filt_step, 2)
                pe.wait_ge(band_ready, 3)

                def weights(s, yg):
                    bank = yg % 2
                    pe.wait_ge(w_evac[bank], (NYG // 2) * s + yg // 2)
                    for r in range(YG):
                        y = yg * YG + r
                        last = nc.tensor.matmul(pw[bank][:, r * CB * FCOLS:(r + 1) * CB * FCOLS],
                                                bands[:, y, :],
                                                filt[:, bass.ds(s * (CB * FCOLS), CB * FCOLS)].bitcast(BF16)[:, 1::2],
                                                start=True, stop=True, skip_group_check=True)
                    last.then_inc(w_ready, 1)

                for yg in range(NYG):
                    weights(0, yg)
                pe.wait_ge(pads_zero, 1)
                with pe.Fori(0, BATCHES // 2) as i:
                    for par in range(2):
                        s = 2 * i + par
                        pe.wait_ge(x_ready, s + 1)
                        for bank in range(2):
                            pe.wait_ge(w_evac[bank], (NYG // 2) * (s + 1))
                        for c in range(CB):
                            pe.wait_ge(h_evac[c], s)
                            for k in range(SHIFTS):
                                n0 = (c * SHIFTS + k) * 2
                                last = nc.tensor.matmul(pc[c][:, 0:B * XH].rearrange("p (b x) -> p b x", b=B),
                                                        toep[par][:, n0:n0 + 2, :].rearrange("p a y -> p (a y)"),
                                                        xpad[par][:, c, :, k:k + XH],
                                                        start=(k == 0), stop=(k == SHIFTS - 1))
                                if k % 2 == 1:
                                    weights(s + 1, after[c][k // 2])
                            last.then_inc(conv_done[par], 1)


def pointwise(nc, d, hs, gate):
    with ExitStack() as ctx:
        def sb(name, shape, dt=F32):
            return ctx.enter_context(nc.sbuf_tensor(name, shape, dt))

        def sem(name):
            return ctx.enter_context(nc.semaphore(name))

        HID = 32
        GROUPS = B * XH // 4
        GPB = GROUPS // B
        ident = sb("ident", [P, P])
        wpw = sb("wpw", [C, C])
        se1 = sb("se1", [C, HID])
        se2 = sb("se2", [HID, C])
        b1 = sb("b1", [HID, 1])
        b2 = sb("b2", [C, 1])
        gam = sb("gam", [C, 1])
        bn = sb("bn", [C, 4])
        bt = sb("bt", [C, 5])
        ht = [sb(f"ht{i}", [C, SL]) for i in range(2)]
        act_out = [sb(f"act_out{i}", [C, H, W]) for i in range(2)]
        sums = sb("sums", [C, GROUPS])
        mean = sb("mean", [C, B])
        hid = sb("hid", [HID, B])
        sig = sb("sig", [C, B])
        pt = [ctx.enter_context(nc.psum_tensor(f"pt{i}", [P, SL], F32)) for i in range(2)]
        pp = [ctx.enter_context(nc.psum_tensor(f"pp{i}", [P, SL], F32)) for i in range(2)]
        ps = [ctx.enter_context(nc.psum_tensor(f"ps{i}", [P, SL], F32)) for i in range(2)]

        p_in = sem("p_in")
        bn_s = sem("bn_s")
        bn_v = sem("bn_v")
        turned = sem("turned")
        t_evac = sem("t_evac")
        mixed = sem("mixed")
        gelu_done = sem("gelu_done")
        g_out = [sem(f"g_out{i}") for i in range(2)]
        se_mean = sem("se_mean")
        se_hid = sem("se_hid")
        se_relu = sem("se_relu")
        se_out = sem("se_out")
        se_sig = sem("se_sig")
        loads = [(ident[:, :], d["ident"]), (wpw[:, :], d["pw_t"]), (se1[:, :], d["se_w1_t"]), (se2[:, :], d["se_w2_t"]),
                 (b1[:, :], d["se_b1"].unsqueeze(1)), (b2[:, :], d["se_b2"].unsqueeze(1)),
                 (gam[:, :], d["gamma"].partition_broadcast(C))]
        loads += [(bn[:, i:i + 1], d["bn2_" + n].unsqueeze(1)) for i, n in enumerate(("gamma", "beta", "mean", "var"))]

        with nc.Block() as block:
            @block.sync
            def _(sp):
                for dst, src in loads:
                    sp.dma_start(dst, src).then_inc(p_in, 16)
                for b in range(B):
                    sp.wait_ge(gelu_done, GPB * (b + 1))
                    sp.dma_start(d["act_scr"][b], act_out[b % 2][:, :, :].rearrange("c y x -> c (y x)")).then_inc(g_out[b % 2], 16)
                for i in range(2):
                    sp.wait_ge(g_out[i], 16 * (B // 2))

            @block.tensor
            def _(pe):
                pe.wait_ge(p_in, 16 * len(loads))

                def mix(g):
                    pe.wait_ge(t_evac, g + 1)
                    if g >= 2:
                        pe.wait_ge(gelu_done, g - 1)
                    nc.tensor.matmul(pp[g % 2][0:C, :], wpw[:, :], ht[g % 2][:, :], start=True, stop=True).then_inc(mixed, 1)

                for g in range(GROUPS):
                    if g >= 2:
                        pe.wait_ge(t_evac, g - 1)
                    for r in range(4):
                        last = nc.tensor.transpose(pt[g % 2][0:C, r * P:(r + 1) * P],
                                                   hs[:, :].rearrange("p (c n) -> p c n", c=C)[:, :, 4 * g + r], ident[:, :])
                    last.then_inc(turned, 1)
                    if g >= 1:
                        mix(g - 1)
                mix(GROUPS - 1)
                pe.wait_ge(se_mean, 2)
                nc.tensor.matmul(ps[0][0:HID, 0:B], se1[:, :], mean[:, :], start=True, stop=True).then_inc(se_hid, 1)
                pe.wait_ge(se_relu, 1)
                nc.tensor.matmul(ps[1][0:C, 0:B], se2[:, :], hid[:, :], start=True, stop=True).then_inc(se_out, 1)

            @block.vector
            def _(dve):
                nc.vector.memset(bt[:, 4:5], BN_EPS).then_inc(bn_s, 1)
                dve.wait_ge(bn_s, 2)
                nc.vector.reciprocal(bt[:, 1:2], bt[:, 0:1]).then_inc(bn_v, 1)
                dve.wait_ge(bn_v, 1)
                nc.vector.tensor_tensor(bt[:, 2:3], bt[:, 1:2], bn[:, 0:1], ALU.mult).then_inc(bn_v, 1)
                dve.wait_ge(bn_v, 2)
                nc.vector.tensor_tensor(bt[:, 1:2], bt[:, 2:3], bn[:, 2:3], ALU.mult).then_inc(bn_v, 1)
                dve.wait_ge(bn_v, 3)
                nc.vector.tensor_tensor(bt[:, 3:4], bn[:, 1:2], bt[:, 1:2], ALU.subtract).then_inc(bn_v, 1)
                for g in range(GROUPS):
                    dve.wait_ge(turned, g + 1)
                    if g >= 2:
                        dve.wait_ge(mixed, g - 1)
                    nc.vector.tensor_copy(ht[g % 2][:, :], pt[g % 2][0:C, :]).then_inc(t_evac, 1)
                dve.wait_ge(gelu_done, GROUPS)
                nc.vector.tensor_reduce(mean[:, :], sums[:, :].rearrange("c (b g) -> c b g", b=B), AX_X, ALU.add).then_inc(se_mean, 1)
                dve.wait_ge(se_mean, 1)
                nc.vector.tensor_scalar(mean[:, :], mean[:, :], 1.0 / L, None, ALU.mult).then_inc(se_mean, 1)
                dve.wait_ge(se_sig, 1)
                nc.vector.tensor_scalar(gate[:, :], sig[:, :], gam[:, 0:1], None, ALU.mult)

            @block.scalar
            def _(act):
                act.wait_ge(p_in, 16 * len(loads))
                act.wait_ge(bn_s, 1)
                nc.scalar.activation(bt[:, 0:1], bn[:, 3:4], ACT.Sqrt, bias=bt[:, 4:5]).then_inc(bn_s, 1)
                act.wait_ge(bn_v, 4)
                for g in range(GROUPS):
                    b, col = g // GPB, g % GPB
                    if b >= 2 and col == 0:
                        act.wait_ge(g_out[b % 2], 16 * (b // 2))
                    act.wait_ge(mixed, g + 1)
                    nc.scalar.activation(act_out[b % 2][:, :, 8 * col:8 * col + 8].rearrange("c y x -> c x y"),
                                         pp[g % 2][0:C, :].rearrange("c (x y) -> c x y", y=H), ACT.Gelu,
                                         bias=bt[:, 3:4], scale=bt[:, 2:3], accum_out=sums[:, g:g + 1]).then_inc(gelu_done, 1)
                act.wait_ge(se_hid, 1)
                nc.scalar.activation(hid[:, :], ps[0][0:HID, 0:B], ACT.Relu, bias=b1[:, 0:1]).then_inc(se_relu, 1)
                act.wait_ge(se_out, 1)
                nc.scalar.activation(sig[:, :], ps[1][0:C, 0:B], ACT.Sigmoid, bias=b2[:, 0:1]).then_inc(se_sig, 1)


def normalise(nc, d, gate):
    RING = 8
    NM = 4
    with ExitStack() as ctx:
        def sb(name, shape, dt=F32):
            return ctx.enter_context(nc.sbuf_tensor(name, shape, dt))

        def sem(name):
            return ctx.enter_context(nc.semaphore(name))

        averager = sb("averager", [C, C])
        lng = sb("lng", [C, 2])
        eps = sb("ln_eps", [C, 1])
        zero = sb("zero", [C, B, HALO])
        h_in = sb("h_in", [C, RING, SL])
        x_in = sb("x_in_ln", [C, RING, SL])
        x1 = sb("x1", [C, RING, SL])
        xc = sb("xc_ln", [C, RING, SL])
        sq = sb("sq", [C, RING, SL])
        ln = sb("ln", [C, RING, SL])
        rs = sb("rs", [C, RING, SL])
        xs = sb("xs", [C, RING, SL])
        xo = sb("xo", [C, RING, SL])
        pm = [ctx.enter_context(nc.psum_tensor(f"pm{i}", [P, SL], F32)) for i in range(NM)]
        pv = [ctx.enter_context(nc.psum_tensor(f"pv{i}", [P, SL], F32)) for i in range(NM)]
        ln_const = sem("ln_const")
        ln_set = sem("ln_set")
        loaded = [sem(f"ln_loaded{i}") for i in range(RING)]
        stored = [sem(f"ln_stored{i}") for i in range(RING)]
        halo = sem("halo")
        added = sem("added")
        mean_ready = sem("mean_ready")
        centred = sem("centred")
        squared = sem("squared")
        var_ready = sem("var_ready")
        ln_ready = sem("ln_ready")
        rs_ready = sem("rs_ready")
        scaled = sem("scaled")
        affine = sem("affine")
        xn = d["xn_scr"]

        with nc.Block() as block:
            @block.sync
            def _(sp):
                sp.dma_start(averager[:, :], d["averager"]).then_inc(ln_const, 16)
                sp.dma_start(lng[:, 0:1], d["ln_g"].unsqueeze(1)).then_inc(ln_const, 16)
                sp.dma_start(lng[:, 1:2], d["ln_b"].unsqueeze(1)).then_inc(ln_const, 16)
                sp.wait_ge(ln_set, 1)
                sp.dma_start(xn[:, :, 0:HALO].rearrange("b c t -> c b t"), zero[:, :, :]).then_inc(halo, 16)
                sp.dma_start(xn[:, :, HALO + L:].rearrange("b c t -> c b t"), zero[:, :, :]).then_inc(halo, 16)

                def load(b, s):
                    r = s % RING
                    after(sp, added, NS * b + s - RING + 1)
                    sp.dma_start(h_in[:, r, :], d["act_scr"][b, :, s * SL:(s + 1) * SL]).then_inc(loaded[r], 16)
                    sp.dma_start(x_in[:, r, :], d["x_tok"][b, :, s * SL:(s + 1) * SL]).then_inc(loaded[r], 16)

                over_slices(sp, (0, load))
                sp.wait_ge(halo, 32)
                for r in range(RING):
                    sp.wait_ge(stored[r], 16 * (B * NS // RING))

            @block.vector
            def _(dve):
                nc.vector.memset(eps[:, :], LN_EPS)
                nc.vector.memset(zero[:, :, :], 0.0).then_inc(ln_set, 1)
                dve.wait_ge(ln_const, 48)

                def add(b, s):
                    r = s % RING
                    dve.wait_ge(loaded[r], 32 * (NS // RING * b + s // RING + 1))
                    after(dve, mean_ready, NS * b + s - RING + 1)
                    nc.vector.scalar_tensor_tensor(x1[:, r, :], h_in[:, r, :], gate[:, bass.ds(b, 1)], x_in[:, r, :],
                                                   ALU.mult, ALU.add).then_inc(added, 1)

                def centre(b, s):
                    r = s % RING
                    dve.wait_ge(mean_ready, NS * b + s + 1)
                    dve.wait_ge(added, NS * b + s + 1)
                    after(dve, scaled, NS * b + s - RING + 1)
                    nc.vector.tensor_tensor(xc[:, r, :], x1[:, r, :], pm[s % NM][0:C, :], ALU.subtract).then_inc(centred, 1)

                def gain(b, s):
                    r = s % RING
                    dve.wait_ge(scaled, NS * b + s + 1)
                    after(dve, stored[r], 16 * (NS // RING * b + s // RING))
                    nc.vector.tensor_scalar(xo[:, r, :], xs[:, r, :], lng[:, 0:1], lng[:, 1:2], ALU.mult, ALU.add).then_inc(affine, 1)

                over_slices(dve, (4, add), (3, centre), (0, gain))

            @block.tensor
            def _(pe):
                pe.wait_ge(ln_const, 48)

                def mean(b, s):
                    pe.wait_ge(added, NS * b + s + 1)
                    after(pe, centred, NS * b + s - NM + 1)
                    nc.tensor.matmul(pm[s % NM][0:C, :], averager[:, :], x1[:, s % RING, :], start=True, stop=True).then_inc(mean_ready, 1)

                def variance(b, s):
                    pe.wait_ge(squared, NS * b + s + 1)
                    after(pe, ln_ready, NS * b + s - NM + 1)
                    nc.tensor.matmul(pv[s % NM][0:C, :], averager[:, :], sq[:, s % RING, :], start=True, stop=True).then_inc(var_ready, 1)

                over_slices(pe, (2, mean), (0, variance))

            @block.scalar
            def _(act):
                act.wait_ge(ln_set, 1)
                load_exp_ln(nc)

                def square(b, s):
                    act.wait_ge(centred, NS * b + s + 1)
                    after(act, var_ready, NS * b + s - RING + 1)
                    nc.scalar.activation(sq[:, s % RING, :], xc[:, s % RING, :], ACT.Square).then_inc(squared, 1)

                def invert(b, s):
                    r = s % RING
                    act.wait_ge(var_ready, NS * b + s + 1)
                    after(act, rs_ready, NS * b + s - RING + 1)
                    nc.scalar.activation(ln[:, r, :], pv[s % NM][0:C, :], ACT.Ln, bias=eps[:, 0:1]).then_inc(ln_ready, 1)
                    after(act, scaled, NS * b + s - RING + 1)
                    act.wait_ge(ln_ready, NS * b + s + 1)
                    nc.scalar.activation(rs[:, r, :], ln[:, r, :], ACT.Exp, scale=-0.5).then_inc(rs_ready, 1)

                def store(b, s):
                    act.wait_ge(affine, NS * b + s + 1)
                    act.dma_start(xn[b, :, HALO + s * SL:HALO + (s + 1) * SL], xo[:, s % RING, :]).then_inc(stored[s % RING], 16)

                over_slices(act, (4, square), (3, invert), (0, store))

            @block.gpsimd
            def _(pool):
                def scale(b, s):
                    r = s % RING
                    pool.wait_ge(rs_ready, NS * b + s + 1)
                    pool.wait_ge(centred, NS * b + s + 1)
                    after(pool, affine, NS * b + s - RING + 1)
                    nc.gpsimd.tensor_tensor(xs[:, r, :], xc[:, r, :], rs[:, r, :], ALU.mult).then_inc(scaled, 1)

                over_slices(pool, (0, scale))


def weights(nc, d, w):
    with ExitStack() as ctx:
        def sb(name, shape, dt=F32):
            return ctx.enter_context(nc.sbuf_tensor(name, shape, dt))

        def sem(name):
            return ctx.enter_context(nc.semaphore(name))

        w_in = sb("w_in", [HALF, DI])
        taps = sb("taps", [HALF, DCONV, DI])
        wx = sb("wx", [HALF, 2, DR + 2 * DS])
        wx_t = sb("wx_t", [DR, DI])
        wdt = sb("wdt", [DR, DI])
        spread_f = sb("spread_f", [HALF, QN * P])
        skip = sb("skip", [HALF, 2])
        ident = sb("ident_w", [HALF, HALF])
        pd = [ctx.enter_context(nc.psum_tensor(f"pd{i}", [P, SL], F32)) for i in range(2)]
        w_loaded = sem("w_loaded")
        w_prod = sem("w_prod")
        a_exp = sem("a_exp")
        loads = [(w_in[:, :], d["w_in"][:, 0:DI]),
                 (taps[:, :, :].rearrange("c k n -> c (k n)"), d["conv_taps"].partition_broadcast(HALF)),
                 (wx[:, :, :], d["w_x"]), (wx_t[:, :], d["w_x_t"]), (wdt[:, :], d["w_dt"]),
                 (spread_f[:, :], d["spread"]), (w["gather"][:, :, :].rearrange("p q n -> p (q n)"), d["gather"]),
                 (w["a"][:, :], d["a_log"]),
                 (w["conv_b"][:, :], d["conv_b"]), (w["dt_b"][:, :], d["dt_b"]), (skip[:, :], d["skip"]), (ident[:, :], d["ident"][0:HALF, 0:HALF])]
        with nc.Block() as block:
            @block.sync
            def _(sp):
                for dst, src in loads:
                    sp.dma_start(dst, src).then_inc(w_loaded, 16)

            @block.scalar
            def _(act):
                act.wait_ge(w_loaded, 16 * len(loads))
                nc.scalar.activation(w["a"][:, :], w["a"][:, :], ACT.Exp).then_inc(a_exp, 1)
                act.wait_ge(a_exp, 1)
                nc.scalar.mul(w["a"][:, :], w["a"][:, :], -1.0)

            @block.tensor
            def _(pe):
                pe.wait_ge(w_loaded, 16 * len(loads))
                for h in range(2):
                    nc.tensor.matmul(pd[h][0:HALF, 0:DI], wx_t[:, h * HALF:(h + 1) * HALF], wdt[:, :], start=True, stop=True).then_inc(w_prod, 1)

            @block.vector
            def _(dve):
                dve.wait_ge(w_loaded, 16 * len(loads))
                for k in range(DCONV):
                    nc.vector.tensor_tensor(w["conv"][:, k, :], w_in[:, :], taps[:, k, :], ALU.mult)
                nc.vector.tensor_copy(w["spread"][:, :, :].rearrange("p q n -> p (q n)"), spread_f[:, :])
                for h in range(2):
                    nc.vector.tensor_scalar(w["skip"][:, h, :], ident[:, :], skip[:, h:h + 1], None, ALU.mult)
                    dve.wait_ge(w_prod, h + 1)
                    nc.vector.tensor_copy(w["dt_bc"][:, h, 0:HALF], pd[h][0:HALF, 0:HALF])
                    nc.vector.tensor_copy(w["dt_bc"][:, h, HALF:P], wx[:, h, DR:])
                    nc.vector.tensor_copy(w["dt"][:, h, :], pd[h][0:HALF, HALF:DI])


def scan(nc, d, w):
    with ExitStack() as ctx:
        def sb(name, shape, dt=F32):
            return ctx.enter_context(nc.sbuf_tensor(name, shape, dt))

        def sem(name):
            return ctx.enter_context(nc.semaphore(name))

        def pair(name, make=None):
            return [(make or sem)(f"{name}{i}") for i in range(2)]

        U_LAG = 1
        NDA, NDB, NHR, NHC = 4, 3, 3, 6
        decay = [sb(f"decay{i}", [P, T]) for i in range(NDA)]
        drive = [sb(f"drive{i}", [P, T]) for i in range(NDB)]
        hring = [sb(f"hring{i}", [P, T]) for i in range(NHR)]
        hc = [sb(f"hc{i}", [P, T]) for i in range(NHC)]
        carry = sb("carry", [P, 2, UNITS])
        ends = sb("ends", [P, 3, UNITS])
        b_rep = pair("b_rep", lambda n: sb(n, [P, T]))
        c_rep = pair("c_rep", lambda n: sb(n, [P, T]))
        stack_dt = pair("stack_dt", lambda n: sb(n, [HALF, 3, T]))
        stack_u = pair("stack_u", lambda n: sb(n, [HALF, 3, T]))
        xn = sb("xn", [C, XN])
        xc = sb("xc", [HALF, 2, T])
        xa = pair("xa", lambda n: sb(n, [HALF, 2, T]))
        y_sb = sb("y_sb", [HALF, T])
        dt3 = [sb(f"dt3_{i}", [HALF, T]) for i in range(3)]
        u3 = [sb(f"u3_{i}", [HALF, T]) for i in range(3)]
        soft = [sb("soft0", [P, T]), sb("soft1", [HALF, T])]
        ramp = pair("ramp", lambda n: sb(n, [HALF, T]))

        dt_ps = [ctx.enter_context(nc.psum_tensor(f"dt_ps{i}", [P, SL], F32)) for i in range(2)]
        u_ps = [ctx.enter_context(nc.psum_tensor(f"u_ps{i}", [P, SL], F32)) for i in range(3)]
        y_ps = ctx.enter_context(nc.psum_tensor("y_ps", [P, 2 * SL], F32))
        prep_ps = ctx.enter_context(nc.psum_tensor("prep_ps", [P, SL], F32))

        zeroed = sem("zeroed")
        dt_spread = sem("dt_spread")
        u_spread = sem("u_spread")
        decay_ready = sem("decay_ready")
        drive_ready = sem("drive_ready")
        scanned = sem("scanned")
        kept = sem("kept")
        carried = sem("carried")
        c_applied = sem("c_applied")
        summed = sem("summed")
        y_ready = sem("y_ready")
        y_stored = sem("y_stored")
        xn_in = sem("xn_in")
        prep_done = sem("prep_done")
        prep_out = sem("prep_out")
        silu_done = sem("silu_done")
        soft_step = sem("soft_step")
        dt_ready = sem("dt_ready")
        u_ready = sem("u_ready")
        split = sem("split")
        bc_stored = sem("bc_stored")
        b_in = pair("b_in")
        c_in = pair("c_in")
        stack_in = pair("stack_in")

        CARRY_AT = 10
        SKIP_AT = 3
        NPREP = 8
        STACKED = 16 * 18
        SILU_AT = 1
        DT_AT = (4, 4, 5, 6, 7, 7, 8, 8)
        CONV_AT = (9, 9, 10, 11, 12, 12, 13, 14, 15, 15, 16, 17, 18, 18, 19, 21)
        CONV_OUT = tuple(CONV_AT[DCONV * g + DCONV - 1] + 1 for g in range(4))
        DT_OUT = tuple(tuple(DT_AT[4 * h + 2 * s + 1] + 1 for s in range(2)) for h in range(2))
        SUM_AT = (6, 12)
        SPLIT_AT = ((8, 9, 10, 11), (14, 15, 16, 17))

        def group(n):
            return n // HU, n % HU // 3, n % 3

        def earlier(lag, u, n, it, dr):
            if isinstance(u, int) and u < lag:
                return None
            if n >= lag:
                return u - lag, n - lag, it, dr
            return u - lag, n - lag + UNITS, it - (1 - dr), 1 - dr

        def run(eng, *tasks):
            for kind, pn in (("conv", 0), ("prep", 0), ("conv", 1)):
                for m in range(UNITS):
                    for has, what in tasks:
                        if has == kind:
                            what(m, pn, 0, pn)
            for n in range(LEAD):
                for kind, what in tasks:
                    if kind == "front":
                        what(n, n, 0, 0)
            with eng.Fori(0, ITERS) as it:
                for dr in range(2):
                    p = 2 * it + dr
                    for m in range(UNITS):
                        n = m + LEAD
                        where = (n, it, dr) if n < UNITS else (n - UNITS, it + dr, 1 - dr)
                        for kind, what in tasks:
                            if kind == "front":
                                what(UNITS * p + n, *where)
                            elif kind == "back":
                                what(m, p, it, dr)
                            elif kind == "prep":
                                what(m, p + 1, it + dr, 1 - dr)
                            else:
                                what(m, p + 2, it + 1, dr)
                    for kind, what in tasks:
                        if kind == "back":
                            what(UNITS, p, it, dr)

        with nc.Block() as block:
            @block.sync
            def _(sp):
                def load_xn(pn, img, tok):
                    wait(sp, prep_done, NPREP * (pn - 1) + 4, not isinstance(pn, int) or pn > 0)
                    sp.dma_start(xn[:, :], d["xn_scr"][img, :, bass.ds(tok, XN)]).then_inc(xn_in, 16)

                def prep_loads(pn, it, dr):
                    sp.wait_ge(prep_out, NPREP * pn + 6)
                    sp.dma_start(d["bc_scr"][dr], soft[0][HALF:P, :]).then_inc(bc_stored, 16)
                    first = isinstance(pn, int)
                    if not first:
                        sp.wait_ge(c_applied, UNITS * (pn - 1))
                    sp.wait_ge(bc_stored, 16 * (pn + 1))
                    for dst, lo, s in ((b_rep, 0, b_in), (c_rep, DS, c_in)):
                        sp.dma_start(dst[dr][:, :], d["bc_scr"][dr][lo:lo + DS, :].partition_broadcast(GC)).then_inc(s[dr], 16)
                    for h in range(2):
                        for parts, i, dst, made, per, step in ((dt3, 0, stack_dt, dt_ready, 1, 1), (u3, 0, stack_u, u_ready, 1, 1),
                                                               (dt3, 1, stack_dt, split, 4, 1), (dt3, 2, stack_dt, split, 4, 2),
                                                               (u3, 1, stack_u, split, 4, 3), (u3, 2, stack_u, split, 4, 4)):
                            sp.wait_ge(made, 2 * per * pn + (per * h + step))
                            if not first and made is dt_ready:
                                sp.wait_ge(u_spread, 2 * (UNITS * (pn - 1) + HU * (h + 1)))
                            for j in range(3):
                                sp.dma_start(dst[h][32 * i:32 * i + 32, j, :], parts[i][32 * j:32 * j + 32, :]).then_inc(stack_in[h], 16)
                        yield h

                def tokens(it, dr):
                    return it % CHUNKS * T if dr == 0 else it % CHUNKS * -T + (CHUNKS - 1) * T

                load_xn(0, 0, tokens(0, 0))
                load_xn(1, 0, tokens(0, 1))
                for _ in prep_loads(0, 0, 0):
                    pass
                load_xn(2, 0, tokens(1, 0))
                with sp.Fori(0, ITERS) as it:
                    for dr in range(2):
                        p = 2 * it + dr
                        later = (it + (1 + dr)) % ITERS
                        img, img3 = it // CHUNKS, later // CHUNKS
                        tok, tok3 = tokens(it, dr), tokens(later, 1 - dr)
                        for h in prep_loads(p + 1, it + dr, 1 - dr):
                            if h == 1:
                                load_xn(p + 3, img3, tok3)
                            sp.wait_ge(y_ready, 2 * p + h + 1)
                            sp.dma_start(d["y_scr"][dr][img, h * HALF:(h + 1) * HALF, bass.ds(tok, T)],
                                         y_sb[:, :]).then_inc(y_stored, 16)
                sp.wait_ge(y_stored, 16 * 4 * ITERS)
                sp.wait_ge(xn_in, 16 * (2 * ITERS + 3))
                for h in range(2):
                    sp.wait_ge(stack_in[h], STACKED * (2 * ITERS + 1))
                sp.wait_ge(b_in[0], 16 * (ITERS + 1))
                sp.wait_ge(c_in[0], 16 * (ITERS + 1))

            @block.tensor
            def _(pe):
                def spread(dst, stack, n, i):
                    h, q, j = group(n)
                    return nc.tensor.matmul(dst[:, :], w["spread"][:, q, :], upper(stack[h][:, j, i * SL:(i + 1) * SL]),
                                            start=True, stop=True)

                def spread_u(i, u, n, it, dr):
                    if (was := earlier(U_LAG, u, n, it, dr)) is not None:
                        v, nv, _, _ = was
                        wait(pe, drive_ready, 2 * v + i - 2, not isinstance(v, int) or 2 * v + i - 2 > 0)
                        spread(u_ps[(2 * nv + i) % 3], stack_u, nv, i).then_inc(u_spread, 1)

                def spread_dt(i, u, n, it, dr):
                    if n % HU == 0 and i == 0:
                        pe.wait_ge(stack_in[n // HU], STACKED * (2 * it + dr + 1))
                    wait(pe, decay_ready, 2 * (u - 1) + i + 1, u)
                    spread(dt_ps[i], stack_dt, n, i).then_inc(dt_spread, 1)

                def back(m, p, it, dr):
                    i = m % 3 - 1
                    if m % HU == SKIP_AT:
                        for s in range(2):
                            nc.tensor.matmul(y_ps[0:HALF, s * SL:(s + 1) * SL], w["skip"][:, m // HU, :],
                                             xa[dr][:, m // HU, s * SL:(s + 1) * SL], start=False, stop=False)
                    if m == UNITS or i < 0:
                        return
                    n0 = m // 3 * 3
                    if i == 0:
                        pe.wait_ge(c_applied, UNITS * p + n0 + 3)
                        if n0 % HU == 0:
                            pe.wait_ge(y_ready, 2 * p + n0 // HU)
                    for n in range(n0, n0 + 3):
                        h, q, j = group(n)
                        last = nc.tensor.matmul(y_ps[32 * j:32 * j + 32, i * SL:(i + 1) * SL], w["gather"][:, q, :],
                                                hc[n % NHC][:, i * SL:(i + 1) * SL], start=(q == 0), stop=(q == QN - 1))
                    if i == 1:
                        last.then_inc(summed, 3)

                def product(k, pn, it, dr):
                    if k < 4 * DCONV:
                        g, tap = divmod(k, DCONV)
                        h, s = divmod(g, 2)
                        if k == 0:
                            pe.wait_ge(xn_in, 16 * (pn + 1))
                        if tap == 0:
                            wait(pe, prep_out, NPREP * pn + g, not isinstance(pn, int) or pn + g > 0)
                        at = s * SL + (tap if dr == 0 else 2 * HALO - tap)
                        mm = nc.tensor.matmul(prep_ps[0:HALF, :], w["conv"][:, tap, h * HALF:(h + 1) * HALF],
                                              xn[:, at:at + SL], start=(tap == 0), stop=(tap == DCONV - 1))
                        if tap == DCONV - 1:
                            mm.then_inc(prep_done, 1)
                        return
                    g, part = divmod(k - 4 * DCONV, 2)
                    h, s = divmod(g, 2)
                    if part == 0:
                        pe.wait_ge(silu_done, pn + 1)
                        pe.wait_ge(prep_out, NPREP * pn + 4 + g)
                    mat, rows = (w["dt"], HALF) if h else (w["dt_bc"], P)
                    mm = nc.tensor.matmul(prep_ps[0:rows, :], mat[:, part, :], xa[dr][:, part, s * SL:(s + 1) * SL],
                                          start=(part == 0), stop=(part == 1))
                    if part == 1:
                        mm.then_inc(prep_done, 1)

                def conv(m, pn, it, dr):
                    for k, at in enumerate(CONV_AT):
                        if at == m:
                            product(k, pn, it, dr)

                def prep(m, pn, it, dr):
                    for k, at in enumerate(DT_AT):
                        if at == m:
                            product(4 * DCONV + k, pn, it, dr)

                run(pe, ("front", partial(spread_u, 0)), ("front", partial(spread_u, 1)), ("front", partial(spread_dt, 0)),
                    ("back", back), ("front", partial(spread_dt, 1)), ("prep", prep), ("conv", conv))

            @block.scalar
            def _(act):
                def front(u, n, it, dr):
                    h, q, j = group(n)
                    col = h * HU + j * QN + q
                    wait(act, scanned, u - NDA + 1, not isinstance(u, int) or u >= NDA)
                    if n == CARRY_AT:
                        act.wait_ge(kept, u - CARRY_AT)
                    for i in range(2):
                        act.wait_ge(dt_spread, 2 * u + i + 1)
                        nc.scalar.activation(decay[n % NDA][:, i * SL:(i + 1) * SL], dt_ps[i][:, :], ACT.Exp,
                                             scale=w["a"][:, col:col + 1]).then_inc(decay_ready, 1)
                    if n == CARRY_AT:
                        _, _, itv, drv = earlier(CARRY_AT + 1, u, n, it, dr)
                        at = drv * UNITS + (itv % CHUNKS) // (CHUNKS - 1) * ((2 - drv) * UNITS)
                        nc.scalar.copy(carry[:, drv, :], ends[:, :, :].rearrange("p d n -> p (d n)")[:, bass.ds(at, UNITS)]).then_inc(carried, 1)
                    if (was := earlier(NDA, u, n, it, dr)) is not None:
                        v, nv, itv, drv = was
                        if nv == 0:
                            wait(act, carried, 2 * itv + drv - 1, not isinstance(v, int))
                        end = T - 1 if drv == 0 else 0
                        nc.scalar.copy(ends[:, drv, nv:nv + 1], hring[nv % NHR][:, end:end + 1]).then_inc(kept, 1)

                def conv(m, pn, it, dr):
                    if m in CONV_OUT:
                        g = CONV_OUT.index(m)
                        h, s = divmod(g, 2)
                        wait(act, silu_done, pn, pn)
                        act.wait_ge(prep_done, NPREP * pn + g + 1)
                        nc.scalar.activation(xc[:, h, s * SL:(s + 1) * SL], prep_ps[0:HALF, :], ACT.Identity,
                                             bias=w["conv_b"][:, h:h + 1]).then_inc(prep_out, 1)

                def prep(m, pn, it, dr):
                    if m == SILU_AT:
                        wait(act, y_ready, 2 * (pn - 1), pn)
                        act.wait_ge(prep_out, NPREP * pn + 4)
                        nc.scalar.activation(xa[dr][:, :, :], xc[:, :, :], ACT.Silu).then_inc(silu_done, 1)
                        load_exp_ln(nc)
                    for h in range(2):
                        if m in DT_OUT[h]:
                            s = DT_OUT[h].index(m)
                            act.wait_ge(prep_done, NPREP * pn + 4 + 2 * h + s + 1)
                            if s == 0:
                                wait(act, dt_ready, 2 * pn + h - 1, not isinstance(pn, int))
                            sl = slice(s * SL, (s + 1) * SL)
                            if h == 0:
                                if s == 0:
                                    wait(act, bc_stored, 16 * pn, pn)
                                nc.scalar.copy(soft[0][HALF:P, sl], prep_ps[HALF:P, :])
                            nc.scalar.activation(soft[h][0:HALF, sl], prep_ps[0:HALF, :], ACT.Abs, bias=w["dt_b"][:, h:h + 1])
                            nc.scalar.activation(ramp[h][:, sl], prep_ps[0:HALF, :], ACT.Relu, bias=w["dt_b"][:, h:h + 1]).then_inc(prep_out, 1)
                            if s == 1:
                                act.wait_ge(prep_out, NPREP * pn + 4 + 2 * h + 2)
                                nc.scalar.activation(soft[h][0:HALF, :], soft[h][0:HALF, :], ACT.Exp, scale=-1.0).then_inc(soft_step, 1)
                                act.wait_ge(soft_step, 2 * (2 * pn + h) + 1)
                                nc.scalar.activation(soft[h][0:HALF, :], soft[h][0:HALF, :], ACT.Ln, bias=1.0).then_inc(soft_step, 1)

                def back(n, p, it, dr):
                    if n == 0 or n % HU:
                        return
                    h = n // HU - 1
                    act.wait_ge(summed, NHC + UNITS * p + n)
                    act.wait_ge(y_stored, 16 * (2 * p + h))
                    nc.scalar.copy(y_sb[:, :], y_ps[0:HALF, :]).then_inc(y_ready, 1)

                act.wait_ge(zeroed, 1)
                load_exp_ln(nc)
                run(act, ("back", back), ("prep", prep), ("conv", conv), ("front", front))

            @block.vector
            def _(dve):
                nc.vector.memset(ends[:, 0:2, :], 0.0)
                nc.vector.memset(carry[:, :, :], 0.0).then_inc(summed, NHC)
                nc.vector.memset(ends[:, 2, :], 0.0).then_inc(zeroed, 1)
                dve.wait_ge(zeroed, 1)

                def front(u, n, it, dr):
                    if (was := earlier(U_LAG, u, n, it, dr)) is None:
                        return
                    v, nv, itv, drv = was
                    if nv == 0:
                        dve.wait_ge(b_in[drv], 16 * (itv + 1))
                    wait(dve, scanned, v - NDB + 1, not isinstance(v, int) or v >= NDB)
                    for i in range(2):
                        dve.wait_ge(u_spread, 2 * v + i + 1)
                        sl = slice(i * SL, (i + 1) * SL)
                        nc.vector.tensor_tensor(drive[nv % NDB][:, sl], u_ps[(2 * nv + i) % 3][:, :], b_rep[drv][:, sl],
                                                ALU.mult).then_inc(drive_ready, 1)
                    if (was := earlier(U_LAG + 1, u, n, it, dr)) is None:
                        return
                    v, nv, itv, drv = was
                    dve.wait_ge(decay_ready, 2 * v + 2)
                    dve.wait_ge(drive_ready, 2 * v + 2)
                    wait(dve, c_applied, v - NHR + 1, not isinstance(v, int) or v >= NHR)
                    wait(dve, kept, v - NHR + 1, not isinstance(v, int) or v >= NHR)
                    if nv == 0:
                        wait(dve, carried, 2 * itv + drv - 1, not isinstance(v, int))
                    r = nv % NHR
                    step = 1 if drv == 0 else -1
                    nc.vector.tensor_tensor_scan(hring[r][:, ::step], decay[nv % NDA][:, ::step],
                                                 drive[nv % NDB][:, ::step], carry[:, drv, nv:nv + 1],
                                                 ALU.mult, ALU.add).then_inc(scanned, 1)

                def prep(m, pn, it, dr):
                    for h in range(2):
                        for i, (parts, ready) in enumerate(((dt3, dt_ready), (u3, u_ready))):
                            for k in range(2):
                                if m == SPLIT_AT[h][2 * i + k]:
                                    count = 4 * (2 * pn + h) + 2 * i + k
                                    dve.wait_ge(ready, 2 * pn + h + 1)
                                    if k == 1:
                                        dve.wait_ge(split, count)
                                    nc.vector.tensor_tensor(parts[k + 1][:, :], parts[k][:, :], upper(parts[k][:, :]),
                                                            ALU.subtract).then_inc(split, 1)

                run(dve, ("front", front), ("prep", prep))

            @block.gpsimd
            def _(pool):
                def front(u, n, it, dr):
                    if (was := earlier(U_LAG + 1, u, n, it, dr)) is None:
                        return
                    v, nv, itv, drv = was
                    if nv == 0:
                        pool.wait_ge(c_in[drv], 16 * (itv + 1))
                    pool.wait_ge(scanned, v + 1)
                    pool.wait_ge(summed, v + 1)
                    r = nv % NHR
                    nc.gpsimd.tensor_tensor(hc[nv % NHC][:, :], hring[r][:, :], c_rep[drv][:, :],
                                            ALU.mult).then_inc(c_applied, 1)

                def prep(m, pn, it, dr):
                    for h in range(2):
                        if m == SUM_AT[h]:
                            pool.wait_ge(soft_step, 2 * (2 * pn + h) + 2)
                            wait(pool, stack_in[1 - h], STACKED * (pn + h), not isinstance(pn, int) or h > 0)
                            nc.gpsimd.tensor_tensor(dt3[0][:, :], soft[h][0:HALF, :], ramp[h][:, :], ALU.add).then_inc(dt_ready, 1)
                        if m == SUM_AT[h] + 1:
                            pool.wait_ge(dt_ready, 2 * pn + h + 1)
                            pool.wait_ge(silu_done, pn + 1)
                            nc.gpsimd.tensor_tensor(u3[0][:, :], dt3[0][:, :], xa[dr][:, h, :], ALU.mult).then_inc(u_ready, 1)

                run(pool, ("front", front), ("prep", prep))


def output(nc, d):
    with ExitStack() as ctx:
        def sb(name, shape, dt=F32):
            return ctx.enter_context(nc.sbuf_tensor(name, shape, dt))

        def sem(name):
            return ctx.enter_context(nc.semaphore(name))

        R = 4
        NO = 4
        w_z = sb("w_z", [C, DI])
        w_out = sb("w_out", [HALF, 2, C])
        yf = sb("yf", [HALF, R, 2, SL])
        yb = sb("yb", [HALF, R, 2, SL])
        xz = sb("xz", [C, R, SL])
        ys = sb("ys", [HALF, R, 2, SL])
        sz = sb("sz", [HALF, R, 2, SL])
        yg = sb("yg", [HALF, R, 2, SL])
        res = sb("res", [C, R, SL])
        pz = [ctx.enter_context(nc.psum_tensor(f"pz{i}", [P, 2 * SL], F32)) for i in range(2)]
        po = [ctx.enter_context(nc.psum_tensor(f"po{i}", [P, SL], F32)) for i in range(NO)]
        o_weights = sem("o_weights")
        o_loaded = [sem(f"o_loaded{i}") for i in range(R)]
        o_stored = [sem(f"o_stored{i}") for i in range(R)]
        y_sum = sem("y_sum")
        z_made = sem("z_made")
        z_silu = sem("z_silu")
        gated = sem("gated")
        projected = sem("projected")
        res_ready = sem("res_ready")
        with nc.Block() as block:
            @block.sync
            def _(sp):
                sp.dma_start(w_z[:, :], d["w_in"][:, DI:2 * DI]).then_inc(o_weights, 16)
                sp.dma_start(w_out[:, :, :], d["w_out"]).then_inc(o_weights, 16)

                def load(b, s):
                    r = s % R
                    after(sp, y_sum, NS * b + s - R + 1)
                    after(sp, z_made, NS * b + s - R + 1)
                    sl = slice(s * SL, (s + 1) * SL)
                    for t, src in ((yf, d["y_scr"][0]), (yb, d["y_scr"][1])):
                        sp.dma_start(t[:, r, :, :], src[b, :, sl].rearrange("(h c) t -> c h t", h=2)).then_inc(o_loaded[r], 16)
                    sp.dma_start(xz[:, r, :], d["xn_scr"][b, :, HALO + s * SL:HALO + (s + 1) * SL]).then_inc(o_loaded[r], 16)

                over_slices(sp, (0, load))
                for r in range(R):
                    sp.wait_ge(o_stored[r], 16 * (B * NS // R))

            @block.gpsimd
            def _(pool):
                def add(b, s):
                    r = s % R
                    pool.wait_ge(o_loaded[r], 48 * (NS // R * b + s // R + 1))
                    after(pool, gated, NS * b + s - R + 1)
                    nc.gpsimd.tensor_tensor(ys[:, r, :, :], yf[:, r, :, :], yb[:, r, :, :], ALU.add).then_inc(y_sum, 1)

                over_slices(pool, (0, add))

            @block.tensor
            def _(pe):
                pe.wait_ge(o_weights, 32)

                def make_z(b, s):
                    pe.wait_ge(o_loaded[s % R], 48 * (NS // R * b + s // R + 1))
                    after(pe, z_silu, NS * b + s - 1)
                    for h in range(2):
                        last = nc.tensor.matmul(pz[s % 2][0:HALF, h * SL:(h + 1) * SL], w_z[:, h * HALF:(h + 1) * HALF],
                                                xz[:, s % R, :], start=True, stop=True)
                    last.then_inc(z_made, 1)

                def project(b, s):
                    pe.wait_ge(gated, NS * b + s + 1)
                    after(pe, res_ready, NS * b + s - NO + 1)
                    for h in range(2):
                        last = nc.tensor.matmul(po[s % NO][0:C, :], w_out[:, h, :], yg[:, s % R, h, :], start=(h == 0), stop=(h == 1))
                    last.then_inc(projected, 1)

                over_slices(pe, (2, make_z), (0, project))

            @block.scalar
            def _(act):
                def gate(b, s):
                    act.wait_ge(z_made, NS * b + s + 1)
                    after(act, gated, NS * b + s - R + 1)
                    nc.scalar.activation(sz[:, s % R, :, :].rearrange("p h t -> p (h t)"), pz[s % 2][0:HALF, :], ACT.Silu).then_inc(z_silu, 1)

                def store(b, s):
                    r = s % R
                    act.wait_ge(projected, NS * b + s + 1)
                    after(act, o_stored[r], 16 * (NS // R * b + s // R))
                    nc.scalar.copy(res[:, r, :], po[s % NO][0:C, :]).then_inc(res_ready, 1)
                    act.wait_ge(res_ready, NS * b + s + 1)
                    act.dma_start(d["out"][b, :, s * SL:(s + 1) * SL], res[:, r, :]).then_inc(o_stored[r], 16)

                over_slices(act, (3, gate), (0, store))

            @block.vector
            def _(dve):
                def multiply(b, s):
                    r = s % R
                    dve.wait_ge(y_sum, NS * b + s + 1)
                    dve.wait_ge(z_silu, NS * b + s + 1)
                    after(dve, projected, NS * b + s - R + 1)
                    nc.vector.tensor_tensor(yg[:, r, :, :], ys[:, r, :, :], sz[:, r, :, :], ALU.mult).then_inc(gated, 1)

                over_slices(dve, (0, multiply))


def mixer_weights(nc, ctx):
    shapes = {"conv": ([HALF, DCONV, DI], F32), "dt_bc": ([HALF, 2, P], F32), "dt": ([HALF, 2, HALF], F32),
              "a": ([P, UNITS], F32),
              "spread": ([HALF, QN, P], BF16), "gather": ([P, QN, 32], F32),
              "conv_b": ([HALF, 2], F32), "dt_b": ([HALF, 2], F32), "skip": ([HALF, 2, HALF], F32)}
    return {n: ctx.enter_context(nc.sbuf_tensor("w_" + n, s, t)) for n, (s, t) in shapes.items()}


def vision_mixer_kernel(nc, d):
    d["act_scr"] = nc.dram_tensor("act_scr", [B, C, L], F32, kind="Internal").ap()
    d["xn_scr"] = nc.dram_tensor("xn_scr", [B, C, L + 2 * HALO], F32, kind="Internal").ap()
    d["y_scr"] = [nc.dram_tensor(f"y_scr{i}", [B, DI, L], F32, kind="Internal").ap() for i in range(2)]
    d["bc_scr"] = [nc.dram_tensor(f"bc_scr{i}", [2 * DS, T], F32, kind="Internal").ap() for i in range(2)]
    with nc.sbuf_tensor("gate", [C, B], F32) as gate:
        with nc.sbuf_tensor("hs", [P, C * B * XH], F32) as hs:
            convolution(nc, d, hs)
            pointwise(nc, d, hs, gate)
        normalise(nc, d, gate)
    with ExitStack() as ctx:
        w = mixer_weights(nc, ctx)
        weights(nc, d, w)
        scan(nc, d, w)
    output(nc, d)


def layout(inputs):
    import numpy as np
    f = {k: np.ascontiguousarray(v) for k, v in inputs.items()}
    x = f["x"]
    d = {}
    d["x_cols"] = x.reshape(B, C, H, XH, 2).transpose(4, 2, 1, 0, 3).reshape(P, C, B, XH)
    d["x_tok"] = x.reshape(B, C, L)
    fp = np.pad(f["L0_conv_plk_filter"].reshape(C, K, K), ((0, 0), (0, 0), (1, 1)))
    cols = np.empty((2, K, C, SHIFTS, 2), np.float32)
    for pi in range(2):
        for po in range(2):
            for s in range(SHIFTS):
                cols[pi, :, :, s, po] = fp[:, :, 2 * s + pi - po + 1].T
    d["filter_cols"] = cols.reshape(FROWS, C * FCOLS)
    band = np.zeros((3, 2, K, 2, 2 * H - 1), np.float32)
    for pi in range(2):
        for dy in range(K):
            band[:, pi, dy, pi, H - 1 + dy - PAD] = 1.0
    d["band"] = band.reshape(3 * FROWS, -1)
    m = np.zeros((3, FROWS, 2), np.float32)
    m[1:, :, 0] = -1.0
    m[2:, :, 1] = -1.0
    d["split_masks"] = m.reshape(3 * FROWS, 2)
    for n in ("gamma", "beta", "mean", "var"):
        d["bn1_" + n] = f["L0_conv_bn1_" + n]
        d["bn2_" + n] = f["L0_conv_bn2_" + n]
    d["ident"] = np.eye(P, dtype=np.float32)
    d["pw_t"] = f["L0_conv_pw_weight"].T
    d["se_w1_t"] = f["L0_conv_se_w1"].T
    d["se_w2_t"] = f["L0_conv_se_w2"].T
    d["se_b1"] = f["L0_conv_se_b1"]
    d["se_b2"] = f["L0_conv_se_b2"]
    d["gamma"] = f["L0_conv_gamma"]
    d["averager"] = np.full((C, C), 1.0 / C, np.float32)
    d["ln_g"] = f["L1_conv_ln_g"]
    d["ln_b"] = f["L1_conv_ln_b"]
    d["w_in"] = f["L1_conv_W_in"]
    d["conv_taps"] = f["L1_conv_conv_w"].T.reshape(-1)
    d["w_x"] = f["L1_conv_W_xproj"].reshape(2, HALF, -1).transpose(1, 0, 2)
    d["w_x_t"] = f["L1_conv_W_xproj"][:, :DR].T
    d["w_dt"] = f["L1_conv_W_dt"]
    d["a_log"] = f["L1_conv_A_log"].reshape(UNITS, P).T
    d["w_out"] = f["L1_conv_W_out"].reshape(2, HALF, C).transpose(1, 0, 2)
    d["conv_b"] = f["L1_conv_conv_b"].reshape(2, HALF).T
    d["dt_b"] = f["L1_conv_b_dt"].reshape(2, HALF).T
    d["skip"] = f["L1_conv_D"].reshape(2, HALF).T
    spread = np.zeros((3, 32, QN, GC, DS), np.float32)
    gather = np.zeros((GC, DS, QN, 32), np.float32)
    for r in range(32):
        spread[:, r, r // GC, r % GC, :] = 1.0
        gather[r % GC, :, r // GC, r] = 1.0
    d["spread"] = spread.reshape(HALF, QN * P)
    d["gather"] = gather.reshape(P, QN * 32)
    return {k: np.ascontiguousarray(v) for k, v in d.items()}


def kernel(**inputs):
    import numpy as np
    import concourse.bacc as bacc
    from concourse.bass_utils import run_bass_kernel_spmd

    nc = bacc.Bacc("TRN2", target_bir_lowering=False, num_devices=1)
    arrays, drams = {}, {}
    for name, a in layout({k: np.asarray(v) for k, v in inputs.items()}).items():
        arrays["in_" + name] = a
        drams[name] = nc.dram_tensor("in_" + name, a.shape, mybir.dt.from_np(a.dtype), kind="ExternalInput").ap()
    drams["out"] = nc.dram_tensor("out", (B, C, L), F32, kind="ExternalOutput").ap()
    vision_mixer_kernel(nc, drams)
    result = run_bass_kernel_spmd(nc, [arrays], core_ids=[0])
    return result.results[0]["out"].reshape(B, C, H, W)
```
